# Optimizing a Trainium2 kernel written in Bass

```python
import numpy as np
import jax
import jax.numpy as jnp

def _softmax(x, axis=-1):
    return jax.nn.softmax(x, axis=axis)
def _gelu(x):
    return jax.nn.gelu(x, approximate=True)
def _silu(x):
    return jax.nn.silu(x)
def _sigmoid(x):
    return jax.nn.sigmoid(x)
def _layernorm(x, axis=-1, eps=1e-5):
    m = jnp.mean(x, axis=axis, keepdims=True)
    v = jnp.var(x, axis=axis, keepdims=True)
    return (x - m) / jnp.sqrt(v + eps)
def _scatter_add(tgt, idx, src, axis=0):
    return tgt.at[idx].add(src)
def _segment_sum(src, seg, n):
    return jax.ops.segment_sum(src, seg, n)

kernel_name = 'mk_conv_preact_d2_conv_nchw384_c98793'

def setup_inputs(seed: int = 0):
    np.random.seed(seed)
    _w = jnp.asarray
    def _rec_inputs():
        import jax
        import jax.numpy as jnp
        _gk = jax.random.key(seed)
        x = -0.0004039 + 1 * jax.random.normal(jax.random.fold_in(_gk, 1), (2, 384, 128, 128), jnp.float32)
        return x
    x = _rec_inputs()
    def _L0_conv_setup():
        import jax, jax.numpy as jnp
        import numpy as np
        B, DIM, HEADS, H, W = (2, 384, 8, 128, 128)

        def _dwconv3x3(x, w):
            return jax.lax.conv_general_dilated(x, w, window_strides=(1, 1), padding='SAME', feature_group_count=x.shape[1], dimension_numbers=('NCHW', 'OIHW', 'NCHW'))

        def _l2norm(t, eps=1e-12):
            n = jnp.sqrt(jnp.sum(t * t, axis=-1, keepdims=True))
            return t / jnp.maximum(n, eps)

        def _topk_softmax(attn, k):
            vals, _ = jax.lax.top_k(attn, k)
            thresh = vals[..., -1:]
            masked = jnp.where(attn >= thresh, attn, -jnp.inf)
            return jax.nn.softmax(masked, axis=-1)
        key = jax.random.key(seed)
        ks = jax.random.split(key, 5)
        s = 0.02
        return {'x': jax.random.normal(ks[0], (B, DIM, H, W), jnp.float32), 'w_qkv': jax.random.normal(ks[1], (3 * DIM, DIM), jnp.float32) * s, 'w_dw': jax.random.normal(ks[2], (3 * DIM, 1, 3, 3), jnp.float32) * s, 'w_proj': jax.random.normal(ks[3], (DIM, DIM), jnp.float32) * s, 'temperature': jnp.ones((HEADS, 1, 1), jnp.float32), 'a1': jnp.array([0.2], jnp.float32), 'a2': jnp.array([0.2], jnp.float32), 'a3': jnp.array([0.2], jnp.float32), 'a4': jnp.array([0.2], jnp.float32)}
    _L0_conv_all = _L0_conv_setup()
    _L0_conv_in = {k: v for k, v in _L0_conv_all.items() if k in ('w_qkv', 'w_dw', 'w_proj', 'temperature', 'a1', 'a2', 'a3', 'a4', )}
    del _L0_conv_all

    def _L1_conv_setup():
        import jax, jax.numpy as jnp
        import numpy as np
        B, DIM, H, W = (2, 384, 256, 256)
        HID = DIM * 1
        P = 8
        key = jax.random.key(seed)
        k0, k1, k2, k3, k4 = jax.random.split(key, 5)
        x = jax.random.normal(k0, (B, DIM, H, W), jnp.float32)
        fft_filter = jax.random.normal(k1, (HID, P, P // 2 + 1), jnp.float32)
        w_in = jax.random.normal(k2, (HID, DIM), jnp.float32) * (1.0 / np.sqrt(DIM))
        w_dw = jax.random.normal(k3, (HID, 1, 3, 3), jnp.float32) * (1.0 / 3.0)
        w_out = jax.random.normal(k4, (DIM, HID // 2), jnp.float32) * (1.0 / np.sqrt(HID // 2))
        return {'x': x, 'fft_filter': fft_filter, 'w_in': w_in, 'w_dw': w_dw, 'w_out': w_out}
    _L1_conv_all = _L1_conv_setup()
    _L1_conv_in = {k: v for k, v in _L1_conv_all.items() if k in ('fft_filter', 'w_in', 'w_dw', 'w_out', )}
    del _L1_conv_all

    return {
        "x": x,
        "L0_conv_w_qkv": _L0_conv_in["w_qkv"],
        "L0_conv_w_dw": _L0_conv_in["w_dw"],
        "L0_conv_w_proj": _L0_conv_in["w_proj"],
        "L0_conv_temperature": _L0_conv_in["temperature"],
        "L0_conv_a1": _L0_conv_in["a1"],
        "L0_conv_a2": _L0_conv_in["a2"],
        "L0_conv_a3": _L0_conv_in["a3"],
        "L0_conv_a4": _L0_conv_in["a4"],
        "L1_conv_fft_filter": _L1_conv_in["fft_filter"],
        "L1_conv_w_in": _L1_conv_in["w_in"],
        "L1_conv_w_dw": _L1_conv_in["w_dw"],
        "L1_conv_w_out": _L1_conv_in["w_out"],
    }

def reference(x, L0_conv_w_qkv, L0_conv_w_dw, L0_conv_w_proj, L0_conv_temperature, L0_conv_a1, L0_conv_a2, L0_conv_a3, L0_conv_a4, L1_conv_fft_filter, L1_conv_w_in, L1_conv_w_dw, L1_conv_w_out):
    import jax
    import jax.numpy as jnp
    def _L0_conv_ref(x, w_qkv, w_dw, w_proj, temperature, a1, a2, a3, a4):
        import jax, jax.numpy as jnp
        import numpy as np
        B, DIM, HEADS, H, W = (2, 384, 8, 128, 128)

        def _dwconv3x3(x, w):
            return jax.lax.conv_general_dilated(x, w, window_strides=(1, 1), padding='SAME', feature_group_count=x.shape[1], dimension_numbers=('NCHW', 'OIHW', 'NCHW'))

        def _l2norm(t, eps=1e-12):
            n = jnp.sqrt(jnp.sum(t * t, axis=-1, keepdims=True))
            return t / jnp.maximum(n, eps)

        def _topk_softmax(attn, k):
            vals, _ = jax.lax.top_k(attn, k)
            thresh = vals[..., -1:]
            masked = jnp.where(attn >= thresh, attn, -jnp.inf)
            return jax.nn.softmax(masked, axis=-1)
        b, c, h, w = x.shape
        qkv = jnp.einsum('bchw,oc->bohw', x, w_qkv)
        qkv = _dwconv3x3(qkv, w_dw)
        q, k, v = jnp.split(qkv, 3, axis=1)
        hd = lambda t: t.reshape(b, HEADS, c // HEADS, h * w)
        q, k, v = (hd(q), hd(k), hd(v))
        q = _l2norm(q)
        k = _l2norm(k)
        C = q.shape[2]
        attn = jnp.einsum('bhcn,bhdn->bhcd', q, k) * temperature
        out = jnp.zeros_like(v)
        for kk, a in zip([C // 2, C * 2 // 3, C * 3 // 4, C * 4 // 5], [a1, a2, a3, a4]):
            p = _topk_softmax(attn, kk)
            out = out + a * jnp.einsum('bhcd,bhdn->bhcn', p, v)
        out = out.reshape(b, c, h, w)
        out = jnp.einsum('bchw,oc->bohw', out, w_proj)
        return out

    def _L1_conv_ref(x, fft_filter, w_in, w_dw, w_out):
        import jax, jax.numpy as jnp
        import numpy as np
        B, DIM, H, W = (2, 384, 256, 256)
        HID = DIM * 1
        P = 8
        b, c, h, w = x.shape
        hid = w_in.shape[0]
        hb, wb = (h // P, w // P)
        t = jnp.einsum('bchw,oc->bohw', x, w_in)
        tp = t.reshape(b, hid, hb, P, wb, P)
        tf = jnp.fft.rfft2(tp, axes=(3, 5))
        tf = tf * fft_filter[None, :, None, :, None, :]
        tp = jnp.fft.irfft2(tf, s=(P, P), axes=(3, 5))
        t = tp.reshape(b, hid, h, w)
        t = jax.lax.conv_general_dilated(t, w_dw, window_strides=(1, 1), padding='SAME', feature_group_count=hid, dimension_numbers=('NCHW', 'OIHW', 'NCHW'))
        x1, x2 = (t[:, :hid // 2], t[:, hid // 2:])
        g = jax.nn.gelu(x1, approximate=False) * x2
        return jnp.einsum('bchw,oc->bohw', g, w_out)

    def _gn(v, G=32, eps=1e-5):
        B_, C_, H_, W_ = v.shape
        g = v.reshape(B_, G, C_ // G, H_, W_)
        m = jnp.mean(g, axis=(2, 3, 4), keepdims=True)
        s = jnp.var(g, axis=(2, 3, 4), keepdims=True)
        return ((g - m) / jnp.sqrt(s + eps)).reshape(v.shape)

    def _ln_c(v, eps=1e-6):
        m = jnp.mean(v, axis=1, keepdims=True)
        s = jnp.var(v, axis=1, keepdims=True)
        return (v - m) / jnp.sqrt(s + eps)

    def _ln_t(v, eps=1e-5):
        m = jnp.mean(v, axis=-1, keepdims=True)
        s = jnp.var(v, axis=-1, keepdims=True)
        return (v - m) / jnp.sqrt(s + eps)

    def _to_tokens(v):
        B_, C_, H_, W_ = v.shape
        return v.reshape(B_, C_, H_ * W_).transpose(0, 2, 1)
    def _from_tokens(t, like):
        B_, C_, H_, W_ = like.shape
        return t.transpose(0, 2, 1).reshape(B_, C_, H_, W_)

    x = x + _L0_conv_ref(_gn(x), L0_conv_w_qkv, L0_conv_w_dw, L0_conv_w_proj, L0_conv_temperature, L0_conv_a1, L0_conv_a2, L0_conv_a3, L0_conv_a4)
    x = x + _L1_conv_ref(_gn(x), L1_conv_fft_filter, L1_conv_w_in, L1_conv_w_dw, L1_conv_w_out)
    return x


_drawn_inputs = setup_inputs


def setup_inputs(seed=0):
    import zlib

    import numpy as np

    out = dict(_drawn_inputs(seed))
    spreads = {'L0_conv_temperature': (1.0, 0.6)}
    factors = {'L0_conv_w_qkv': 8.0, 'L0_conv_w_dw': 8.0, 'L0_conv_w_proj': 8.0}
    for name, (base, spread) in spreads.items():
        noise = np.random.default_rng([zlib.crc32(name.encode()), seed]).standard_normal(out[name].shape)
        drawn = base * np.exp(spread * noise) if base else spread * noise
        out[name] = jnp.asarray(drawn.astype(out[name].dtype))
    for name, factor in factors.items():
        out[name] = (out[name] * factor).astype(out[name].dtype)
    return out
```

```python
from contextlib import ExitStack

import numpy as np

import concourse.bass as bass
from concourse import mybir

F32 = mybir.dt.float32
F32R = mybir.dt.float32r
ALU = mybir.AluOpType
ACT = mybir.ActivationFunctionType
AX_X = mybir.AxisListType.X

P = 128
B = 2
CH = 384
T = CH // P
W = 128
HEADS = 8
HC = CH // HEADS
PAIRS = HEADS // 2
SLOT = 64
R = 8
CW = R * W
HALF = CW // 2
UR, UW = R + 2, W + 2
QT = 3 * CH // P
KT = 2 * CH // P
GROUP = 12
BLK = P // R
NBLK = W // BLK
GN_EPS = 1e-5
TOPK = [HC // 2, HC * 2 // 3, HC * 3 // 4, HC * 4 // 5]
RING = 5
LAG = RING - 1
LOWEST = -3.0e38
ACT_TAPS = [4, 0, 2]
DVE_TAPS = [1, 3, 5, 6, 7, 8]


def after(engine, semaphore, value):
    if not isinstance(value, int) or value > 0:
        engine.wait_ge(semaphore, value)


def end_waits(engine, passed):
    engine.sem_inc(passed, 1)


def over_chunks(engine, chunks, body, alone=1):
    for c in range(2 * alone):
        body(c, c % 2)
    with engine.Fori(alone, chunks // 2 - 1) as pair:
        for s in (0, 1):
            body(2 * pair + s, s)
    for c in (chunks - 2, chunks - 1):
        body(c, c % 2)


def spectrum_constants():
    fwd, inv, sel = [], [], []
    y, x = np.meshgrid(np.arange(R), np.arange(R), indexing="ij")
    for ky in range(R // 2 + 1):
        edge = ky in (0, R // 2)
        for kx in range(R // 2 + 1 if edge else R):
            angle = 2 * np.pi * ((kx * y + ky * x) % R) / R
            alone = edge and kx in (0, R // 2)
            pick = np.zeros((R, R // 2 + 1))
            pick[kx, ky] += 0.5
            pick[(-kx) % R if edge else kx, ky] += 0.5
            for part in (np.cos(angle),) if alone else (np.cos(angle), -np.sin(angle)):
                fwd.append(part)
                inv.append(part * (1 if alone else 2) / R**2)
                sel.append(pick.ravel())
    fwd, inv, sel = np.array(fwd), np.array(inv), np.array(sel)
    n = len(fwd)
    forward = np.zeros((R, 2, R, 2, n))
    inverse = np.zeros((2, n, R, 2, R))
    for p in range(2):
        forward[:, p, :, p, :] = fwd.transpose(1, 2, 0)
        inverse[p, :, :, p, :] = inv
    spread = np.concatenate([sel, sel], 0).T
    return (forward.reshape(P, P).astype(np.float32), inverse.reshape(P, P).astype(np.float32),
            np.ascontiguousarray(spread, np.float32))


def norm_coefficients(nc, ctx, block, name, partials, group_avg, psum, out):
    def sem(what):
        return ctx.enter_context(nc.semaphore(f"{name}_{what}"))

    step, avg_in, avg_out, dev_in, dev_out, root = (
        sem(w) for w in ("step", "avg_in", "avg_out", "dev_in", "dev_out", "root"))
    own = ctx.enter_context(nc.sbuf_tensor(f"{name}_own", [P, B, 2], F32))
    dev = ctx.enter_context(nc.sbuf_tensor(f"{name}_dev", [P, B], F32))
    var = ctx.enter_context(nc.sbuf_tensor(f"{name}_var", [P, B], F32))
    std = ctx.enter_context(nc.sbuf_tensor(f"{name}_std", [P, B], F32))
    tmp = ctx.enter_context(nc.sbuf_tensor(f"{name}_tmp", [P, B], F32))

    def vector(dve):
        count = [0]

        def then_wait(instruction):
            count[0] += 1
            instruction.then_inc(step, 1)
            dve.wait_ge(step, count[0])

        for b in range(B):
            then_wait(nc.vector.bn_aggr(own[:, b, :], partials[:, b, :]))
        dve.sem_inc(avg_in, 1)
        dve.wait_ge(avg_out, 1)
        then_wait(nc.vector.tensor_copy(out[:, :, 0], psum[:, 0:2 * B].rearrange("p (b s) -> p b s", b=B)[:, :, 0]))
        then_wait(nc.vector.tensor_copy(var[:], psum[:, 0:2 * B].rearrange("p (b s) -> p b s", b=B)[:, :, 1]))
        then_wait(nc.vector.tensor_tensor(tmp[:], own[:, :, 0], out[:, :, 0], ALU.subtract))
        then_wait(nc.vector.tensor_tensor(dev[:], tmp[:], tmp[:], ALU.mult))
        dve.sem_inc(dev_in, 1)
        dve.wait_ge(dev_out, 1)
        then_wait(nc.vector.tensor_tensor(tmp[:], var[:], psum[:, 8:8 + B], ALU.add))
        nc.vector.tensor_scalar(var[:], tmp[:], GN_EPS, None, ALU.add).then_inc(root, 1)
        dve.wait_ge(root, 2)
        then_wait(nc.vector.reciprocal(std[:], dev[:]))
        then_wait(nc.vector.tensor_tensor(tmp[:], std[:], std[:], ALU.mult))
        then_wait(nc.vector.tensor_tensor(dev[:], tmp[:], var[:], ALU.mult))
        then_wait(nc.vector.tensor_scalar(tmp[:], dev[:], -0.5, 1.5, ALU.mult, ALU.add))
        then_wait(nc.vector.tensor_tensor(out[:, :, 1], tmp[:], std[:], ALU.mult))

    def tensor(pe):
        pe.wait_ge(avg_in, 1)
        nc.tensor.matmul(psum[:, 0:2 * B], group_avg[:], own[:].rearrange("p b s -> p (b s)"),
                         start=True, stop=True).then_inc(avg_out, 1)
        pe.wait_ge(dev_in, 1)
        nc.tensor.matmul(psum[:, 8:8 + B], group_avg[:], dev[:], start=True, stop=True).then_inc(dev_out, 1)

    def scalar(act):
        act.wait_ge(root, 1)
        nc.scalar.activation(dev[:], var[:], ACT.Sqrt).then_inc(root, 1)

    return vector, tensor, scalar


def two_layers(nc, x, wqkv, wdw0, wproj, temperature, a1, a2, a3, a4, filt, win, wdw1, wout,
               identity_in, group_in, forward_in, inverse_in, spread_in, out):
    H = x.shape[2]
    C = H // R
    xv, ov = (a.rearrange("b (p t) h w -> b p t (h w)", t=T) for a in (x, out))
    v_d = nc.dram_tensor("v_scratch", [B, T, P, (H + R) * W], F32).ap()
    x1_d = nc.dram_tensor("x1_scratch", [B, P, T, H * W], F32).ap()
    gram_d = nc.dram_tensor("gram_scratch", [B, PAIRS, 2 * HC, 2 * HC], F32).ap()
    norm_d = nc.dram_tensor("norm_scratch", [B, KT * P], F32).ap()
    mix_d = nc.dram_tensor("mix_scratch", [B, CH, CH], F32).ap()

    with ExitStack() as whole:
        def keep(name, shape):
            return whole.enter_context(nc.sbuf_tensor(name, shape, F32))

        banks = whole.enter_context(nc.psum_tensor("banks", [P, 8, 512], F32))
        gn0, gn1 = keep("gn0", [P, B, 2]), keep("gn1", [P, B, 2])
        group_avg = keep("group_avg", [P, P])
        identity = keep("identity", [P, P])
        gram = keep("gram", [P, B, PAIRS * 2 * HC])
        squares = keep("squares", [P, B, KT, C + 1])

        with ExitStack() as ctx:
            def sb(name, shape):
                return ctx.enter_context(nc.sbuf_tensor(name, shape, F32))

            def sem(name):
                return ctx.enter_context(nc.semaphore(name))

            xs = sb("st_x", [P, 2, T, CW])
            partials = sb("st_partials", [P, B, C * T * 12])
            st_loaded = [sem("st_loaded0"), sem("st_loaded1")]
            consts_loaded, st_used, passed = sem("st_consts"), sem("st_used"), sem("st_passed")
            block = ctx.enter_context(nc.Block())
            vector, tensor, scalar = norm_coefficients(nc, ctx, block, "gn0", partials, group_avg,
                                                       banks[:, 0, :], gn0)

            @block.sync
            def _(sp):
                sp.dma_start(group_avg[:], group_in).then_inc(consts_loaded, 16)
                sp.dma_start(identity[:], identity_in).then_inc(consts_loaded, 16)
                for b in range(B):
                    def load(c, s):
                        after(sp, st_used, b * C + c - 1)
                        end_waits(sp, passed)
                        sp.dma_start(xs[:, s], xv[b][:, :, bass.ds(c * CW, CW)]).then_inc(st_loaded[s], 16)
                    over_chunks(sp, C, load)
                sp.wait_ge(consts_loaded, 32)

            @block.vector
            def _(dve):
                for b in range(B):
                    def stats(c, s):
                        dve.wait_ge(st_loaded[s], (c - s + b * C) * 8 + 16)
                        for t in range(T):
                            for h in range(2):
                                last = nc.vector.bn_stats(
                                    partials[:, b, bass.ds(c * (T * 12) + (t * 2 + h) * 6, 6)],
                                    xs[:, s, t, h * HALF:(h + 1) * HALF])
                        last.then_inc(st_used, 1)
                    over_chunks(dve, C, stats)
                dve.wait_ge(st_used, B * C)
                vector(dve)

            @block.tensor
            def _(pe):
                pe.wait_ge(consts_loaded, 32)
                tensor(pe)

            @block.scalar
            def _(act):
                scalar(act)

        with ExitStack() as ctx:
            def sb(name, shape, dtype=F32):
                return ctx.enter_context(nc.sbuf_tensor(name, shape, dtype))

            def sem(name):
                return ctx.enter_context(nc.semaphore(name))

            w_high, w_low = sb("wq_high", [P, T, 3 * CH], F32R), sb("wq_low", [P, T, 3 * CH], F32R)
            taps = sb("taps0", [P, QT, 9])
            xs = sb("a_x", [P, T, CW])
            x_high, x_low = sb("x_high", [P, 2, T, CW], F32R), sb("x_low", [P, 2, T, CW], F32R)
            u = sb("u", [P, RING, UR, UW])
            carry = sb("carry", [P, QT, 2, W])
            z = sb("z", [P, 3, 2, CW])
            y = sb("y", [P, RING, CW])
            junk = sb("junk", [P, CW])
            qkT = sb("qkT", [P, 2, R, CH])
            up = [banks[:, 2 * i:2 * i + 2, :].rearrange("p a n -> p (a n)") for i in range(2)]
            turned = banks[:, 4:6, :].rearrange("p a n -> p (a n)")
            gram_ps = banks[0:2 * HC, 6, 0:PAIRS * 2 * HC]

            weights_loaded, split = sem("a_weights"), sem("a_split")
            x_loaded = sem("a_x_loaded")
            passed = sem("a_passed")
            cleared = sem("a_cleared")
            normalised = sem("a_normalised")
            xn_ready = sem("a_xn")
            up_ready = sem("a_up")
            u_written = sem("a_u")
            carried_out = sem("a_carried_out")
            carried_in = sem("a_carried_in")
            products = sem("a_products")
            added = sem("a_added")
            tap_done = sem("a_tap")
            cut = sem("a_cut")
            y_ready = sem("a_y")
            squared = sem("a_squared")
            turned_ready = sem("a_turned")
            turned_kept = sem("a_turned_kept")
            gram_ready = sem("a_gram")
            gram_added = sem("a_gram_added")
            v_stored = [sem(f"a_v{i}") for i in range(T)]
            block = ctx.enter_context(nc.Block())

            NC = C + 1
            CHAIN = len(DVE_TAPS)

            def shifted(t, tap, rows):
                dy, dx = tap // 3, tap % 3
                return u[:, t % RING, dy:dy + rows, dx:dx + W]

            def image(ap, rows):
                return ap[:, 0:rows * W].rearrange("p (r w) -> p r w", w=W)

            def wait_slot_read(engine, g, t):
                before = max(k for k in range(-QT, t) if k % QT % RING == t % RING)
                g, tile = (g, before) if before >= 0 else (g - 1, before + QT)
                if tile < KT:
                    after(engine, turned_ready, g * KT + tile + 1)
                    after(engine, squared, g * KT + tile + 1)
                else:
                    after(engine, v_stored[tile - KT], (g + 1) * 16)

            @block.sync
            def _(sp):
                raw = z[:].rearrange("p a b n -> p (a b n)")[:, 0:T * 3 * CH].rearrange("p (t o) -> p t o", t=T)
                sp.dma_start(raw, wqkv.rearrange("(p t) o -> p t o", t=T)).then_inc(weights_loaded, 16)
                sp.dma_start(taps[:], wdw0.rearrange("(t p) k -> p t k", p=P)).then_inc(weights_loaded, 16)

                def load(b, c):
                    after(sp, xn_ready, b * C + c)
                    end_waits(sp, passed)
                    sp.dma_start(xs[:], xv[b][:, :, bass.ds(c * CW, CW)]).then_inc(x_loaded, 16)

                def store_v(b, c, rows):
                    for t in range(KT, QT):
                        sp.wait_ge(y_ready, (b * NC + c) * QT + t + 1)
                        end_waits(sp, passed)
                        sp.dma_start(v_d[b, t - KT][:, bass.ds(c * CW, rows * W)],
                                     y[:, t % RING, 0:rows * W]).then_inc(v_stored[t - KT], 16)

                load(0, 0)
                for b in range(B):
                    def chunk(c, s):
                        if not (isinstance(c, int) and c == C - 1):
                            load(b, c + 1)
                        elif b + 1 < B:
                            load(b + 1, 0)
                        store_v(b, c, R)
                    over_chunks(sp, C, chunk)
                    store_v(b, C, 1)
                for t in range(T):
                    sp.wait_ge(v_stored[t], B * NC * 16)

            @block.tensor
            def _(pe):
                pe.wait_ge(split, 2)
                for b in range(B):
                    def turn(c, t, rows):
                        g = b * NC + c
                        pe.wait_ge(y_ready, g * QT + t + 1)
                        after(pe, turned_kept, g * KT + t)
                        for i in range(rows):
                            last = nc.tensor.transpose(turned[:, i * P:(i + 1) * P],
                                                       y[:, t % RING, i * W:(i + 1) * W], identity[:])
                        last.then_inc(turned_ready, 1)

                    def multiply_gram(c, rows):
                        g = b * NC + c
                        pe.wait_ge(turned_kept, (g + 1) * KT)
                        after(pe, gram_added, g)
                        for p in range(PAIRS):
                            pair = slice(p * 2 * HC, (p + 1) * 2 * HC)
                            for i in range(rows):
                                last = nc.tensor.matmul(gram_ps[:, pair], qkT[:, 0, i, pair], qkT[:, 1, i, pair],
                                                        start=(i == 0), stop=(i == rows - 1))
                        last.then_inc(gram_ready, 1)

                    def chunk(c, s):
                        first = isinstance(c, int) and c == 0
                        pe.wait_ge(xn_ready, b * C + c + 1)
                        for t in range(QT):
                            m = (b * C + c) * QT + t
                            after(pe, carried_out, m - 1)
                            for h in range(2):
                                to = up[(s * QT + t) % 2][:, h * HALF:(h + 1) * HALF]
                                for k in range(T):
                                    for i, (w, xp) in enumerate(((w_high, x_high), (w_low, x_high), (w_high, x_low))):
                                        last = nc.tensor.matmul(
                                            to, w[:, k, t * P:(t + 1) * P], xp[:, s, k, h * HALF:(h + 1) * HALF],
                                            start=(k == 0 and i == 0), stop=(k == T - 1 and i == 2))
                            last.then_inc(up_ready, 1)
                            if t >= LAG:
                                turn(c, t - LAG, R)
                            elif QT - LAG + t < KT and not first:
                                turn(c - 1, QT - LAG + t, R)
                            elif t == KT - QT + LAG and not first:
                                multiply_gram(c - 1, R)
                    over_chunks(pe, C, chunk)
                    for t in range(QT - LAG, KT):
                        turn(C - 1, t, R)
                    multiply_gram(C - 1, R)
                    for t in range(KT):
                        turn(C, t, 1)
                    multiply_gram(C, 1)

            @block.scalar
            def _(act):
                act.wait_ge(weights_loaded, 32)
                act.wait_ge(cleared, 2)
                for b in range(B):
                    def keep(c, t, rows):
                        g = b * NC + c
                        act.wait_ge(turned_ready, g * KT + t + 1)
                        after(act, gram_ready, g)
                        nc.scalar.copy(qkT[:, t // T, 0:rows, t % T * P:(t % T + 1) * P],
                                       turned[:, 0:rows * P].rearrange("p (r d) -> p r d", d=P)).then_inc(turned_kept, 1)

                    def square(c, t, rows):
                        q = (b * NC + c) * KT + t
                        act.wait_ge(y_ready, (b * NC + c) * QT + t + 1)
                        after(act, squared, q)
                        nc.scalar.activation(junk[:, 0:rows * W], y[:, t % RING, 0:rows * W], ACT.Square,
                                             accum_out=squares[:, b, t, bass.ds(c, 1)]).then_inc(squared, 1)

                    def multiply(c, t, rows):
                        g = b * NC + c
                        n = g * QT + t
                        act.wait_ge(u_written, n + 1)
                        act.wait_ge(carried_in, n + 1)
                        wait_slot_read(act, g, t)
                        after(act, added, 2 * (n - 2))
                        for k, tap in enumerate(ACT_TAPS):
                            to = y[:, t % RING, :] if k == 0 else z[:, t % 3, k - 1, :]
                            nc.scalar.activation(image(to, rows), shifted(t, tap, rows), ACT.Copy,
                                                 scale=taps[:, t, tap:tap + 1]).then_inc(products, 1)

                    def chunk(c, s):
                        first = isinstance(c, int) and c == 0
                        for t in range(QT):
                            g = b * NC + c
                            n = g * QT + t
                            m = (b * C + c) * QT + t
                            act.wait_ge(up_ready, m + 1)
                            after(act, y_ready, n - LAG + 1)
                            rows_in = up[(s * QT + t) % 2].rearrange("p (r w) -> p r w", w=W)
                            nc.scalar.copy(u[:, t % RING, 2:UR, 1:1 + W], rows_in).then_inc(u_written, 1)
                            act.wait_ge(carried_in, n + 1)
                            nc.scalar.copy(carry[:, t, :, :], rows_in[:, R - 2:R, :]).then_inc(carried_out, 1)
                            if t > LAG:
                                keep(c, t - LAG - 1, R)
                            elif QT - LAG + t - 1 < KT and not first:
                                keep(c - 1, QT - LAG + t - 1, R)
                            if t >= LAG:
                                square(c, t - LAG, R)
                            elif QT + t - LAG < KT and not first:
                                square(c - 1, QT + t - LAG, R)
                            multiply(c, t, R)
                    over_chunks(act, C, chunk)
                    for t in range(QT):
                        if t < KT + LAG - QT:
                            square(C - 1, QT + t - LAG, R)
                        if t == 0:
                            for i in range(QT - LAG - 1, KT):
                                keep(C - 1, i, R)
                        multiply(C, t, 1)
                        if 3 <= t < KT + 3:
                            square(C, t - 3, 1)
                            keep(C, t - 3, 1)

            @block.gpsimd
            def _(pool):
                nc.gpsimd.memset(u[:], 0.0).then_inc(cleared, 1)
                nc.gpsimd.memset(gram[:], 0.0).then_inc(cleared, 1)
                pool.wait_ge(cleared, 2)

                def carry_in(b, c, t):
                    n = (b * NC + c) * QT + t
                    after(pool, y_ready, n - LAG + 1)
                    top = u[:, t % RING, 0:2, 1:1 + W]
                    if isinstance(c, int) and c == 0:
                        nc.gpsimd.memset(top, 0.0).then_inc(carried_in, 1)
                        return
                    pool.wait_ge(carried_out, (b * C + c - 1) * QT + t + 1)
                    if isinstance(c, int) and c == C:
                        pool.wait_ge(u_written, n)
                        nc.gpsimd.memset(u[:, t % RING, 2, 1:1 + W], 0.0).then_inc(u_written, 1)
                    end_waits(pool, passed)
                    nc.gpsimd.tensor_copy(top, carry[:, t, :, :]).then_inc(carried_in, 1)

                def split_low(i, s):
                    pool.wait_ge(normalised, 2 * i + 2)
                    after(pool, up_ready, (i - 1) * QT)
                    nc.gpsimd.tensor_tensor(x_low[:, s], xs[:], x_high[:, s].bitcast(F32), ALU.subtract).then_inc(xn_ready, 1)

                split_low(0, 0)
                carry_in(0, 0, 0)
                for b in range(B):
                    def steps(c, s, rows):
                        fixed = isinstance(c, int)
                        for t in range(QT):
                            n = (b * NC + c) * QT + t
                            if t + 1 < QT:
                                carry_in(b, c, t + 1)
                            elif not (fixed and c == C):
                                carry_in(b, c + 1, 0)
                            elif b + 1 < B:
                                carry_in(b + 1, 0, 0)
                            pool.wait_ge(products, 3 * n + 3)
                            to = y[:, t % RING, 0:rows * W]
                            for k in range(2):
                                nc.gpsimd.tensor_tensor(to, to, z[:, t % 3, k, 0:rows * W], ALU.add).then_inc(added, 1)
                                pool.wait_ge(added, 2 * n + k + 1)
                            if t == 5:
                                if not (fixed and c >= C - 1):
                                    split_low(b * C + c + 1, 1 - s)
                                elif c == C and b + 1 < B:
                                    split_low((b + 1) * C, 0)

                    over_chunks(pool, C, lambda c, s: steps(c, s, R))
                    steps(C, 0, 1)

            @block.vector
            def _(dve):
                dve.wait_ge(weights_loaded, 32)
                raw = z[:].rearrange("p a b n -> p (a b n)")[:, 0:T * 3 * CH].rearrange("p (t o) -> p t o", t=T)
                nc.vector.tensor_copy(w_high[:], raw).then_inc(split, 1)
                dve.wait_ge(split, 1)
                nc.vector.tensor_tensor(w_low[:], raw, w_high[:].bitcast(F32), ALU.subtract).then_inc(split, 1)
                dve.wait_ge(cleared, 2)

                def normalise(b, c, s):
                    i = b * C + c
                    dve.wait_ge(x_loaded, 16 * (i + 1))
                    after(dve, up_ready, (i - 1) * QT)
                    for to in (x_high[:, s], xs[:]):
                        nc.vector.tensor_scalar(to, xs[:], gn0[:, b, 0:1], gn0[:, b, 1:2],
                                                ALU.subtract, ALU.mult).then_inc(normalised, 1)

                def add_gram(b, c):
                    dve.wait_ge(gram_ready, b * NC + c + 1)
                    after(dve, gram_added, b * NC + c)
                    total = gram[0:2 * HC, b, :]
                    nc.vector.tensor_tensor(total, total, gram_ps, ALU.add).then_inc(gram_added, 1)

                normalise(0, 0, 0)
                for b in range(B):
                    def steps(c, s, rows):
                        fixed = isinstance(c, int)
                        for t in range(QT):
                            n = (b * NC + c) * QT + t
                            dve.wait_ge(added, 2 * n + 2)
                            to = image(y[:, t % RING, :], rows)
                            for k, tap in enumerate(DVE_TAPS):
                                if k:
                                    dve.wait_ge(tap_done, n * (CHAIN - 1) + k)
                                done = tap_done if k < CHAIN - 1 else cut if fixed and c == 0 else y_ready
                                nc.vector.scalar_tensor_tensor(
                                    to, shifted(t, tap, rows), taps[:, t, tap:tap + 1], to,
                                    ALU.mult, ALU.add).then_inc(done, 1)
                            if fixed and c == 0:
                                dve.wait_ge(cut, b * QT + t + 1)
                                nc.vector.memset(to[:, 0, :], 0.0).then_inc(y_ready, 1)
                            if t == 5 and not (fixed and c == 0):
                                add_gram(b, c - 1)
                            if t == 4:
                                if not (fixed and c >= C - 1):
                                    normalise(b, c + 1, 1 - s)
                                elif c == C and b + 1 < B:
                                    normalise(b + 1, 0, 0)

                    over_chunks(dve, C, lambda c, s: steps(c, s, R))
                    steps(C, 0, 1)
                    add_gram(b, C)

        with ExitStack() as ctx:
            def sb(name, shape):
                return ctx.enter_context(nc.sbuf_tensor(name, shape, F32))

            def sem(name):
                return ctx.enter_context(nc.semaphore(name))

            NB = B * PAIRS
            K4 = len(TOPK)
            ssq, rn, nt0, nt1 = (sb(n, [P, B * KT]) for n in ("ssq", "rn", "nt0", "nt1"))
            qn = sb("qn", [P, B, PAIRS])
            kn = sb("kn", [P, B, PAIRS, HC])
            temp = sb("temp", [P, PAIRS])
            gains = sb("gains", [P, K4])
            qk = sb("qk", [P, NB, HC])
            scaled = sb("scaled", [P, NB, HC])
            logits = sb("logits", [P, NB, HC])
            left = sb("left", [P, NB, HC])
            tops = sb("tops", [P, NB, 40])
            lowered = sb("lowered", [P, NB])
            expd = sb("expd", [P, NB, HC])
            masked = sb("masked", [P, K4, NB, HC])
            sums = sb("sums", [P, K4, NB])
            shares = sb("shares", [P, K4, NB])
            mixed = sb("mixed", [P, NB, HC])
            diag = sb("diag", [P, NB, P])
            wp = sb("wp", [P, PAIRS, CH])
            mt = sb("mt", [P, NB, CH])
            t_moved = sem("t_moved")
            t_loaded, t_norm, t_back = sem("t_loaded"), sem("t_norm"), sem("t_back")
            t_zeroed, t_chain, t_root = sem("t_zeroed"), sem("t_chain"), sem("t_root")
            t_exp, t_diag, t_mt, t_mt_kept, t_stored = (
                sem(n) for n in ("t_exp", "t_diag", "t_mt", "t_mt_kept", "t_stored"))
            block = ctx.enter_context(nc.Block())

            @block.sync
            def _(sp):
                with nc.allow_non_contiguous_dma(reason="tables of a few hundred numbers"):
                    wpv = wproj.rearrange("(p s i) o -> s i p o", s=2, i=HC)
                    tv = temperature.rearrange("(p s) a b -> s (a b) p", s=2)
                    sp.wait_ge(t_zeroed, 1)
                    for s in range(2):
                        sp.dma_start(wp[s * SLOT:s * SLOT + HC], wpv[s]).then_inc(t_loaded, 16)
                        sp.dma_start(temp[s * SLOT:(s + 1) * SLOT], tv[s].to_broadcast([SLOT, PAIRS])).then_inc(t_loaded, 16)
                    for i, a in enumerate((a1, a2, a3, a4)):
                        sp.dma_start(gains[:, i:i + 1], a.rearrange("(a b) -> a b", a=1).to_broadcast([P, 1])).then_inc(t_loaded, 16)
                    for b in range(B):
                        sp.dma_start(gram_d[b].rearrange("r i j -> i r j"),
                                     gram[0:2 * HC, b, :].rearrange("p (r j) -> p r j", r=PAIRS)).then_inc(t_moved, 16)
                    sp.wait_ge(t_norm, 1)
                    for b in range(B):
                        sp.dma_start(norm_d[b].rearrange("(t p) -> p t", p=P), rn[:, b * KT:(b + 1) * KT]).then_inc(t_back, 16)
                    sp.wait_ge(t_back, 16 * B)
                    sp.wait_ge(t_moved, 16 * B)
                    for n in range(NB):
                        for s in range(2):
                            own = slice(s * HC, (s + 1) * HC)
                            sp.dma_start(qk[s * SLOT:s * SLOT + HC, n, :], gram_d[n // PAIRS, n % PAIRS][own, own]
                                         ).then_inc(t_moved, 16)
                    for b in range(B):
                        nq = norm_d[b, 0:CH].rearrange("(p s i) -> s i p", s=2, i=HC)
                        nk = norm_d[b, CH:2 * CH].rearrange("(a p s i) -> s a p i", a=1, s=2, i=HC)
                        for s in range(2):
                            sp.dma_start(qn[s * SLOT:s * SLOT + HC, b, :], nq[s]).then_inc(t_back, 16)
                            sp.dma_start(kn[s * SLOT:(s + 1) * SLOT, b], nk[s].to_broadcast([SLOT, PAIRS, HC])).then_inc(t_back, 16)
                for n in range(NB):
                    b, p = n // PAIRS, n % PAIRS
                    sp.wait_ge(t_mt_kept, n + 1)
                    for s in range(2):
                        row = (2 * p + s) * HC
                        sp.dma_start(mix_d[b, row:row + HC, :], mt[s * SLOT:s * SLOT + HC, n, :]).then_inc(t_stored, 16)
                sp.wait_ge(t_stored, 16 * 2 * NB)

            @block.scalar
            def _(act):
                act.wait_ge(t_root, 1)
                nc.scalar.activation(nt0[:], ssq[:], ACT.Sqrt).then_inc(t_root, 1)
                act.wait_ge(t_exp, 1)
                for n in range(NB):
                    last = nc.scalar.activation(expd[:, n, :], logits[:, n, :], ACT.Exp, bias=lowered[:, n:n + 1])
                last.then_inc(t_exp, 1)
                for n in range(NB):
                    act.wait_ge(t_mt, n + 1)
                    nc.scalar.copy(mt[:, n, :], banks[:, n, 0:CH]).then_inc(t_mt_kept, 1)

            @block.tensor
            def _(pe):
                pe.wait_ge(t_diag, 1)
                pe.wait_ge(t_loaded, 16 * 8)
                for n in range(NB):
                    nc.tensor.matmul(banks[:, n, 0:CH], diag[:, n, :], wp[:, n % PAIRS, :],
                                     start=True, stop=True).then_inc(t_mt, 1)

            @block.vector
            def _(dve):
                count = [0]

                def then_wait(instruction):
                    count[0] += 1
                    instruction.then_inc(t_chain, 1)
                    dve.wait_ge(t_chain, count[0])

                def settle(instructions):
                    for i in instructions:
                        i.then_inc(t_chain, 1)
                        count[0] += 1
                    dve.wait_ge(t_chain, count[0])

                settle([nc.vector.memset(a[:], 0.0) for a in (wp, qn, qk, diag)])
                dve.sem_inc(t_zeroed, 1)
                then_wait(nc.vector.reduce_sum(rn[:], squares[:].rearrange("p b t c -> p (b t) c"), AX_X))
                nc.vector.tensor_scalar(ssq[:], rn[:], 1e-24, None, ALU.max).then_inc(t_root, 1)
                dve.wait_ge(t_root, 2)
                then_wait(nc.vector.reciprocal(nt1[:], nt0[:]))
                then_wait(nc.vector.tensor_tensor(nt0[:], nt1[:], nt1[:], ALU.mult))
                then_wait(nc.vector.tensor_tensor(rn[:], nt0[:], ssq[:], ALU.mult))
                then_wait(nc.vector.tensor_scalar(nt0[:], rn[:], -0.5, 1.5, ALU.mult, ALU.add))
                nc.vector.tensor_tensor(rn[:], nt0[:], nt1[:], ALU.mult).then_inc(t_norm, 1)
                dve.wait_ge(t_loaded, 16 * 8)
                dve.wait_ge(t_back, 16 * 5 * B)
                knv = kn[:].rearrange("p b r d -> p (b r) d")
                dve.wait_ge(t_moved, 16 * (B + 2 * NB))
                then_wait(nc.vector.tensor_tensor(scaled[:], qk[:], knv, ALU.mult))
                settle([nc.vector.tensor_scalar(logits[:, n, :], scaled[:, n, :], qn[:, n // PAIRS, n % PAIRS:n % PAIRS + 1],
                                                temp[:, n % PAIRS:n % PAIRS + 1], ALU.mult, ALU.mult) for n in range(NB)])
                for e in range(5):
                    now = logits if e == 0 else left
                    settle([nc.vector.max(tops[:, n, 8 * e:8 * e + 8], now[:, n, :]) for n in range(NB)])
                    if e < 4:
                        settle([nc.vector.match_replace(left[:, n, :], tops[:, n, 8 * e:8 * e + 8], now[:, n, :], LOWEST)
                                for n in range(NB)])
                nc.vector.tensor_scalar(lowered[:], tops[:, :, 0], -1.0, None, ALU.mult).then_inc(t_exp, 1)
                dve.wait_ge(t_exp, 2)
                settle([nc.vector.scalar_tensor_tensor(masked[:, i, n, :], logits[:, n, :], tops[:, n, k - 1:k],
                                                       expd[:, n, :], ALU.is_ge, ALU.mult)
                        for i, k in enumerate(TOPK) for n in range(NB)])
                then_wait(nc.vector.reduce_sum(sums[:].rearrange("p a n -> p (a n)"),
                                               masked[:].rearrange("p a n d -> p (a n) d"), AX_X))
                then_wait(nc.vector.reciprocal(shares[:], sums[:]))
                settle([nc.vector.tensor_scalar(sums[:, i, :], shares[:, i, :], gains[:, i:i + 1], None, ALU.mult)
                        for i in range(K4)])
                settle([nc.vector.tensor_scalar(mixed[:, n, :], masked[:, 0, n, :], sums[:, 0, n:n + 1], None, ALU.mult)
                        for n in range(NB)])
                for i in range(1, K4):
                    settle([nc.vector.scalar_tensor_tensor(mixed[:, n, :], masked[:, i, n, :], sums[:, i, n:n + 1],
                                                           mixed[:, n, :], ALU.mult, ALU.add) for n in range(NB)])
                settle([nc.vector.tensor_copy(diag[s * SLOT:s * SLOT + HC, :, s * SLOT:s * SLOT + HC],
                                              mixed[s * SLOT:s * SLOT + HC]) for s in range(2)])
                dve.sem_inc(t_diag, 1)

        with ExitStack() as ctx:
            def sb(name, shape):
                return ctx.enter_context(nc.sbuf_tensor(name, shape, F32))

            def sem(name):
                return ctx.enter_context(nc.semaphore(name))

            mix = sb("mix", [P, B, T, CH])
            vs = sb("vs", [P, 2, T, CW])
            xs = sb("p_x", [P, 2, T, CW])
            partials = sb("p_partials", [P, B, C * T * 12])
            up = [banks[:, 2 * i:2 * i + 2, :].rearrange("p a n -> p (a n)") for i in range(2)]
            mix_loaded, passed = sem("p_mix"), sem("p_passed")
            v_loaded, x_loaded, x1_stored = ([sem(f"p_{n}{i}") for i in range(2)] for n in ("v", "x", "x1"))
            mixed_ready = sem("p_mixed")
            x1_ready = sem("p_x1_ready")
            counted = sem("p_counted")
            block = ctx.enter_context(nc.Block())
            vector, tensor, scalar = norm_coefficients(nc, ctx, block, "gn1", partials, group_avg,
                                                       banks[:, 7, :], gn1)

            @block.sync
            def _(sp):
                for b in range(B):
                    sp.dma_start(mix[:, b], mix_d[b].rearrange("(k p) o -> p k o", p=P)).then_inc(mix_loaded, 16)
                for b in range(B):
                    def load(c, s):
                        i = b * C + c
                        after(sp, mixed_ready, (i - 1) * T)
                        end_waits(sp, passed)
                        sp.dma_start(vs[:, s], v_d[b].rearrange("t p n -> p t n")[:, :, bass.ds(c * CW + W, CW)]
                                     ).then_inc(v_loaded[s], 16)
                        after(sp, counted, (i - 1) * T)
                        end_waits(sp, passed)
                        after(sp, x1_stored[s], (b * C + c - s) * 8)
                        end_waits(sp, passed)
                        sp.dma_start(xs[:, s], xv[b][:, :, bass.ds(c * CW, CW)]).then_inc(x_loaded[s], 16)
                    over_chunks(sp, C, load)

            @block.tensor
            def _(pe):
                pe.wait_ge(mix_loaded, 16 * B)
                for b in range(B):
                    def chunk(c, s):
                        pe.wait_ge(v_loaded[s], (b * C + c - s) * 8 + 16)
                        for m in range(T):
                            i = (b * C + c) * T + m
                            after(pe, x1_ready, i - 1)
                            for h in range(2):
                                for k in range(T):
                                    last = nc.tensor.matmul(
                                        up[(s * T + m) % 2][:, h * HALF:(h + 1) * HALF],
                                        mix[:, b, k, m * P:(m + 1) * P], vs[:, s, k, h * HALF:(h + 1) * HALF],
                                        start=(k == 0), stop=(k == T - 1))
                            last.then_inc(mixed_ready, 1)
                    over_chunks(pe, C, chunk)
                tensor(pe)

            @block.scalar
            def _(act):
                for b in range(B):
                    def store(c, s):
                        act.wait_ge(x1_ready, (b * C + c + 1) * T)
                        end_waits(act, passed)
                        act.dma_start(x1_d[b][:, :, bass.ds(c * CW, CW)], xs[:, s]).then_inc(x1_stored[s], 16)
                    over_chunks(act, C, store)
                for s in range(2):
                    act.wait_ge(x1_stored[s], B * C * 8)
                scalar(act)

            @block.vector
            def _(dve):
                for b in range(B):
                    def chunk(c, s):
                        dve.wait_ge(x_loaded[s], (b * C + c - s) * 8 + 16)
                        for m in range(T):
                            i = (b * C + c) * T + m
                            dve.wait_ge(mixed_ready, i + 1)
                            nc.vector.tensor_tensor(xs[:, s, m, :], up[(s * T + m) % 2], xs[:, s, m, :],
                                                    ALU.add).then_inc(x1_ready, 1)
                            dve.wait_ge(x1_ready, i + 1)
                            for h in range(2):
                                last = nc.vector.bn_stats(
                                    partials[:, b, bass.ds(c * (T * 12) + (m * 2 + h) * 6, 6)],
                                    xs[:, s, m, h * HALF:(h + 1) * HALF])
                            last.then_inc(counted, 1)
                    over_chunks(dve, C, chunk)
                dve.wait_ge(counted, B * C * T)
                vector(dve)

        with ExitStack() as ctx:
            def sb(name, shape):
                return ctx.enter_context(nc.sbuf_tensor(name, shape, F32))

            def sem(name):
                return ctx.enter_context(nc.semaphore(name))

            NC = C + 1
            H2 = CH // 2
            REST = H2 - P
            wi = sb("wi", [P, T, CH])
            wo = sb("wo", [P, 2, CH])
            taps = sb("taps1", [P, T, 9])
            forward, inverse = sb("forward", [P, P]), sb("inverse", [P, P])
            half_filter = sb("half_filter", [R * (R // 2 + 1), CH])
            spread = sb("spread", [R * (R // 2 + 1), P])
            filt_sb = sb("filt_sb", [P, CH])
            xw = sb("f_xw", [P, 2, T, CW])
            xn = sb("f_xn", [P, 2, T, CW])
            xr = sb("f_xr", [P, 2, T, CW])
            pixels = sb("pixels", [P, 2, CH])
            spectra = sb("spectra", [P, 2, CH])
            u = sb("f_u", [P, 2, T, UR, UW])
            z = sb("f_z", [P, T, 2, CW])
            y = sb("f_y", [P, 2, T, CW])
            aside = sb("aside", [REST, CW])

            f_weights, filter_ready, f_cleared = sem("f_weights"), sem("f_filter"), sem("f_cleared")
            passed = sem("f_passed")
            x_loaded = [sem("f_x0"), sem("f_x1")]
            r_loaded = [sem("f_r0"), sem("f_r1")]
            o_stored = [sem("f_o0"), sem("f_o1")]
            xn_ready = sem("f_xn_ready")
            s1_ready = sem("f_s1")
            pixels_kept = sem("f_pixels")
            coef_ready = sem("f_coef")
            filtered = sem("f_filtered")
            inv_ready = sem("f_inv")
            u_written = sem("f_u_written")
            window_ready = sem("f_window")
            products = sem("f_products")
            added = sem("f_added")
            tap_done = sem("f_tap")
            y_ready = sem("f_y_ready")
            gelu_done = sem("f_gelu")
            gated = sem("f_gated")
            out_ready = sem("f_out")
            summed = sem("f_summed")
            block = ctx.enter_context(nc.Block())
            CHAIN = len(DVE_TAPS)
            s1_ps = [banks[:, i, 0:CH] for i in (0, 1)]
            coef_ps = [banks[:, i, 0:CH] for i in (2, 3)]
            inv_ps = [banks[:, i, 0:CH] for i in (4, 5)]
            out_ps = banks[:, 6:8, :].rearrange("p a n -> p (a n)")

            def shifted(t, s, tap, rows):
                dy, dx = tap // 3, tap % 3
                return u[:, s, t, dy:dy + rows, dx:dx + W]

            def rows_of(ap, rows):
                return ap[:, 0:rows * W].rearrange("p (r w) -> p r w", w=W)

            def over_slots(engine, body):
                over_chunks(engine, C, body, alone=2)
                for k in (C, C + 1, C + 2):
                    body(k, k % 2)

            def alive(k, chunk, end):
                return not isinstance(k, int) or 0 <= chunk < end

            def stored(b, i, c=0, s=0):
                return (b * (C // 2 + (1 - i)) * 16) + (c - s) * 8

            def height(k, chunk):
                return 1 if isinstance(k, int) and chunk == C else R

            @block.sync
            def _(sp):
                loads = [(wi[:], win.rearrange("(p t) o -> p t o", t=T)), (wo[:, 0, :], wout[0:P]),
                         (wo[0:REST, 1, :], wout[P:H2]), (taps[:], wdw1.rearrange("(t p) k -> p t k", p=P)),
                         (forward[:], forward_in), (inverse[:], inverse_in),
                         (half_filter[:], filt), (spread[:], spread_in)]
                for to, source in loads:
                    sp.dma_start(to, source).then_inc(f_weights, 16)
                sp.wait_ge(f_cleared, 1)

                def load(b, c, s):
                    after(sp, xn_ready, (b * C + c - 1) * T)
                    end_waits(sp, passed)
                    sp.dma_start(xw[:, s], x1_d[b][:, :, bass.ds(c * CW, CW)]).then_inc(x_loaded[s], 16)

                load(0, 0, 0)
                for b in range(B):
                    def slot(k, s):
                        if alive(k, k + 1, C):
                            load(b, k + 1, 1 - s)
                        elif isinstance(k, int) and k == C and b + 1 < B:
                            load(b + 1, 0, 0)
                        if alive(k, k - 1, NC):
                            rows = height(k, k - 1)
                            after(sp, o_stored[1 - s], stored(b, 1 - s, k - 1, 1 - s))
                            end_waits(sp, passed)
                            if isinstance(k, int) and k == 1:
                                sp.dma_start(xr[:, 1 - s, :, W:], x1_d[b][:, :, 0:CW - W]).then_inc(r_loaded[1 - s], 16)
                            else:
                                sp.dma_start(xr[:, 1 - s, :, 0:rows * W],
                                             x1_d[b][:, :, bass.ds((k - 1) * CW - W, rows * W)]).then_inc(r_loaded[1 - s], 16)
                        if alive(k, k - 2, NC):
                            rows = height(k, k - 2)
                            sp.wait_ge(summed, (b * NC + k - 1) * T)
                            end_waits(sp, passed)
                            if isinstance(k, int) and k == 2:
                                sp.dma_start(ov[b][:, :, 0:CW - W], xr[:, s, :, W:]).then_inc(o_stored[s], 16)
                            else:
                                sp.dma_start(ov[b][:, :, bass.ds((k - 2) * CW - W, rows * W)],
                                             xr[:, s, :, 0:rows * W]).then_inc(o_stored[s], 16)
                    over_slots(sp, slot)
                for i in range(2):
                    sp.wait_ge(o_stored[i], stored(B, i))

            @block.tensor
            def _(pe):
                pe.wait_ge(f_weights, 16 * 8)
                nc.tensor.matmul(banks[:, 7, 0:CH], spread[:], half_filter[:], start=True, stop=True).then_inc(filter_ready, 1)
                pe.wait_ge(filter_ready, 2)
                for b in range(B):
                    def slot(k, s):
                        on = alive(k, k, C)
                        if on:
                            pe.wait_ge(xn_ready, (b * C + k + 1) * T)
                        for j in range(NBLK + 2):
                            q = (b * C + k) * NBLK + j
                            if on and j < NBLK:
                                after(pe, pixels_kept, q - 1)
                                for t in range(T):
                                    last = nc.tensor.matmul(
                                        s1_ps[j % 2],
                                        xn[:, s, t, j * P:(j + 1) * P],
                                        wi[:, t, :], start=(t == 0), stop=(t == T - 1))
                                last.then_inc(s1_ready, 1)
                            if on and 1 <= j < NBLK + 1:
                                pe.wait_ge(pixels_kept, q)
                                after(pe, filtered, q - 2)
                                nc.tensor.matmul(coef_ps[(j - 1) % 2], forward[:], pixels[:, (j - 1) % 2, :],
                                                 start=True, stop=True).then_inc(coef_ready, 1)
                            if on and j >= 2:
                                pe.wait_ge(filtered, q - 1)
                                after(pe, u_written, q - 3)
                                for t in range(T):
                                    last = nc.tensor.matmul(
                                        inv_ps[j % 2][:, t * P:(t + 1) * P], spectra[:, j % 2, t * P:(t + 1) * P],
                                        inverse[:], start=True, stop=True)
                                last.then_inc(inv_ready, 1)
                            if j in (4, 6, 8) and alive(k, k - 2, NC):
                                m = (j - 4) // 2
                                g = b * NC + k - 2
                                rows = height(k, k - 2)
                                if m == 0:
                                    pe.wait_ge(gated, g + 1)
                                after(pe, summed, g * T + m)
                                for h in range(2 if rows == R else 1):
                                    n = HALF if rows == R else W
                                    nc.tensor.matmul(out_ps[:, h * HALF:h * HALF + n], wo[:, 0, m * P:(m + 1) * P],
                                                     y[:, s, 0, h * HALF:h * HALF + n], start=True, stop=False)
                                    last = nc.tensor.matmul(out_ps[:, h * HALF:h * HALF + n], wo[0:REST, 1, m * P:(m + 1) * P],
                                                            y[0:REST, s, 2, h * HALF:h * HALF + n], start=False, stop=True)
                                last.then_inc(out_ready, 1)
                    over_slots(pe, slot)

            @block.scalar
            def _(act):
                act.wait_ge(filter_ready, 1)
                nc.scalar.copy(filt_sb[:], banks[:, 7, 0:CH]).then_inc(filter_ready, 1)
                act.wait_ge(f_weights, 16 * 8)
                act.wait_ge(f_cleared, 1)
                for b in range(B):
                    def slot(k, s):
                        on = alive(k, k, C)
                        for j in range(NBLK + 2):
                            q = (b * C + k) * NBLK + j
                            if on and j < NBLK:
                                act.wait_ge(s1_ready, q + 1)
                                after(act, coef_ready, q - 1)
                                nc.scalar.copy(pixels[:, j % 2, :], s1_ps[j % 2]).then_inc(pixels_kept, 1)
                            if on and j >= 2:
                                if j == 2:
                                    past = 0 if isinstance(k, int) and k == 0 else 1
                                    after(act, y_ready, (b * NC + k - past) * T)
                                    after(act, window_ready, b * NC + k)
                                act.wait_ge(inv_ready, q - 1)
                                at = 1 + (j - 2) * BLK
                                nc.scalar.copy(u[:, s, :, 2:UR, at:at + BLK],
                                               inv_ps[j % 2].rearrange("p (t r w) -> p t r w", t=T, r=R)
                                               ).then_inc(u_written, 1)
                            if j == 2 and alive(k, k - 2, NC):
                                g = b * NC + k - 2
                                n = height(k, k - 2) * W
                                act.wait_ge(y_ready, (g + 1) * T)
                                after(act, gated, g)
                                nc.scalar.activation(y[:, s, 0, 0:n], y[:, s, 0, 0:n], ACT.Gelu)
                                nc.scalar.activation(y[0:REST, s, 2, 0:n], y[0:REST, s, 2, 0:n], ACT.Gelu)
                                nc.scalar.copy(aside[:, 0:n], y[REST:2 * REST, s, 2, 0:n]).then_inc(gelu_done, 1)
                        if alive(k, k, NC):
                            rows = height(k, k)
                            g = b * NC + k
                            act.wait_ge(u_written, (b * C + k) * NBLK + NBLK if rows == R else (b + 1) * C * NBLK)
                            act.wait_ge(window_ready, g + 1)
                            after(act, out_ready, (g - 1) * T if alive(k, k - 2, NC) else b * NC * T)
                            for t in range(T):
                                n = g * T + t
                                after(act, added, 2 * (n - T + 1))
                                for i, tap in enumerate(ACT_TAPS):
                                    to = y[:, s, t, :] if i == 0 else z[:, t, i - 1, :]
                                    nc.scalar.activation(rows_of(to, rows), shifted(t, s, tap, rows), ACT.Copy,
                                                         scale=taps[:, t, tap:tap + 1]).then_inc(products, 1)
                    over_slots(act, slot)

            @block.gpsimd
            def _(pool):
                nc.gpsimd.memset(u[:], 0.0)
                nc.gpsimd.memset(xr[:], 0.0).then_inc(f_cleared, 1)
                pool.wait_ge(f_cleared, 1)
                for b in range(B):
                    def slot(k, s):
                        if not alive(k, k, NC):
                            return
                        g = b * NC + k
                        rows = height(k, k)
                        past = g if isinstance(k, int) and k == 0 else g - 1
                        after(pool, y_ready, past * T)
                        after(pool, products, past * T * 3)
                        if isinstance(k, int) and k == 0:
                            nc.gpsimd.memset(u[:, s, :, 0:2, :], 0.0).then_inc(window_ready, 1)
                        else:
                            pool.wait_ge(u_written, (b * C + k) * NBLK)
                            end_waits(pool, passed)
                            if rows == 1:
                                nc.gpsimd.memset(u[:, s, :, 2, :], 0.0)
                            nc.gpsimd.tensor_copy(u[:, s, :, 0:2, :], u[:, 1 - s, :, R:UR, :]).then_inc(window_ready, 1)
                        for t in range(T):
                            n = g * T + t
                            pool.wait_ge(products, 3 * n + 3)
                            for i in range(2):
                                nc.gpsimd.tensor_tensor(y[:, s, t, 0:rows * W], y[:, s, t, 0:rows * W],
                                                        z[:, t, i, 0:rows * W], ALU.add).then_inc(added, 1)
                                pool.wait_ge(added, 2 * n + i + 1)
                    over_slots(pool, slot)

            @block.vector
            def _(dve):
                dve.wait_ge(f_weights, 16 * 8)
                dve.wait_ge(filter_ready, 2)

                def normalise(b, c, s):
                    dve.wait_ge(x_loaded[s], (c - s + b * C) * 8 + 16)
                    after(dve, s1_ready, (b * C + c - 1) * NBLK)
                    for t in range(T):
                        nc.vector.tensor_scalar(
                            xn[:, s, t, :].rearrange("p (j r w) -> p r j w", r=R, w=BLK),
                            xw[:, s, t, :].rearrange("p (r j w) -> p r j w", r=R, w=BLK),
                            gn1[:, b, 0:1], gn1[:, b, 1:2], ALU.subtract, ALU.mult).then_inc(xn_ready, 1)

                normalise(0, 0, 0)
                for b in range(B):
                    def slot(k, s):
                        steps = [(t, i) for t in range(T) for i in range(CHAIN)]
                        for j in range(NBLK):
                            q = (b * C + k) * NBLK + j
                            if alive(k, k, C):
                                dve.wait_ge(coef_ready, q + 1)
                                after(dve, inv_ready, q - 1)
                                nc.vector.tensor_tensor(spectra[:, j % 2, :], coef_ps[j % 2], filt_sb[:],
                                                        ALU.mult).then_inc(filtered, 1)
                            if alive(k, k - 1, NC):
                                g = b * NC + k - 1
                                rows = height(k, k - 1)
                                for t, i in steps[j * len(steps) // NBLK:(j + 1) * len(steps) // NBLK]:
                                    n = g * T + t
                                    to = rows_of(y[:, 1 - s, t, :], rows)
                                    if i == 0:
                                        dve.wait_ge(added, 2 * n + 2)
                                    else:
                                        dve.wait_ge(tap_done, n * (CHAIN - 1) + i)
                                    tap = DVE_TAPS[i]
                                    nc.vector.scalar_tensor_tensor(
                                        to, shifted(t, 1 - s, tap, rows), taps[:, t, tap:tap + 1], to,
                                        ALU.mult, ALU.add).then_inc(tap_done if i < CHAIN - 1 else y_ready, 1)
                            if alive(k, k - 2, NC):
                                g = b * NC + k - 2
                                size = height(k, k - 2) * W
                                if j == 3:
                                    dve.wait_ge(gelu_done, g + 1)
                                    nc.vector.tensor_tensor(y[:, s, 0, 0:size], y[:, s, 0, 0:size], y[:, s, 1, 0:size], ALU.mult)
                                    nc.vector.tensor_tensor(y[0:REST, s, 2, 0:size], y[0:REST, s, 2, 0:size],
                                                            aside[:, 0:size], ALU.mult).then_inc(gated, 1)
                                if j in (5, 6, 7):
                                    m = j - 5
                                    if m == 0:
                                        dve.wait_ge(r_loaded[s], stored(b, s, k - 2, s) + 16)
                                    dve.wait_ge(out_ready, g * T + m + 1)
                                    nc.vector.tensor_tensor(xr[:, s, m, 0:size], out_ps[:, 0:size], xr[:, s, m, 0:size],
                                                            ALU.add).then_inc(summed, 1)
                            if j == 1:
                                if alive(k, k + 1, C):
                                    normalise(b, k + 1, 1 - s)
                                elif isinstance(k, int) and k == C + 1 and b + 1 < B:
                                    normalise(b + 1, 0, 0)
                    over_slots(dve, slot)


def kernel(x, L0_conv_w_qkv, L0_conv_w_dw, L0_conv_w_proj, L0_conv_temperature, L0_conv_a1, L0_conv_a2,
           L0_conv_a3, L0_conv_a4, L1_conv_fft_filter, L1_conv_w_in, L1_conv_w_dw, L1_conv_w_out):
    import concourse.bacc as _bacc
    from concourse.bass_utils import run_bass_kernel_spmd as _run

    half = CH // 2
    hidden = [*range(0, P), *range(half, half + P), *range(P, half), *range(half + P, CH)]
    columns = [T * m + t for t in range(T) for m in range(P)]
    forward, inverse, spread = spectrum_constants()
    group = (np.arange(P)[:, None] // (GROUP // T) == np.arange(P)[None, :] // (GROUP // T))
    arrays = {
        "x": x,
        "wqkv": L0_conv_w_qkv.T,
        "wdw0": L0_conv_w_dw.reshape(3 * CH, 9),
        "wproj": L0_conv_w_proj.T[:, columns],
        "temperature": L0_conv_temperature,
        "a1": L0_conv_a1, "a2": L0_conv_a2, "a3": L0_conv_a3, "a4": L0_conv_a4,
        "filt": L1_conv_fft_filter.reshape(CH, -1).T[:, hidden],
        "win": L1_conv_w_in.T[:, hidden],
        "wdw1": L1_conv_w_dw.reshape(CH, 9)[hidden],
        "wout": L1_conv_w_out.T[:, columns],
        "identity": np.eye(P, dtype=np.float32),
        "group": group.astype(np.float32) * np.float32(T / GROUP),
        "forward": forward, "inverse": inverse, "spread": spread,
    }
    arrays = {f"in_{name}": np.ascontiguousarray(a) for name, a in arrays.items()}
    nc = _bacc.Bacc("TRN2", target_bir_lowering=False, num_devices=1)
    args = [nc.dram_tensor(name, a.shape, mybir.dt.from_np(a.dtype), kind="ExternalInput").ap()
            for name, a in arrays.items()]
    out = nc.dram_tensor("out", x.shape, F32, kind="ExternalOutput").ap()
    two_layers(nc, *args, out)
    r = _run(nc, [arrays], core_ids=[0])
    return r.results[0]["out"]
```

```python
from contextlib import ExitStack

import numpy as np

import concourse.bass as bass
from concourse import mybir

F32 = mybir.dt.float32
F32R = mybir.dt.float32r
ALU = mybir.AluOpType
ACT = mybir.ActivationFunctionType
AX_X = mybir.AxisListType.X

P = 128
B = 2
CH = 384
T = CH // P
W = 128
HEADS = 8
HC = CH // HEADS
PAIRS = HEADS // 2
SLOT = 64
R = 8
CW = R * W
HALF = CW // 2
UR, UW = R + 2, W + 2
QT = 3 * CH // P
KT = 2 * CH // P
GROUP = 12
BLK = P // R
NBLK = W // BLK
GN_EPS = 1e-5
TOPK = [HC // 2, HC * 2 // 3, HC * 3 // 4, HC * 4 // 5]
RING = 5
LAG = RING - 1
LOWEST = -3.0e38
ACT_TAPS = [4, 0, 2]
DVE_TAPS = [1, 3, 5, 6, 7, 8]


def after(engine, semaphore, value):
    if not isinstance(value, int) or value > 0:
        engine.wait_ge(semaphore, value)


def end_waits(engine, passed):
    engine.sem_inc(passed, 1)


def over_chunks(engine, chunks, body, alone=1):
    for c in range(2 * alone):
        body(c, c % 2)
    with engine.Fori(alone, chunks // 2 - 1) as pair:
        for s in (0, 1):
            body(2 * pair + s, s)
    for c in (chunks - 2, chunks - 1):
        body(c, c % 2)


def spectrum_constants():
    fwd, inv, sel = [], [], []
    y, x = np.meshgrid(np.arange(R), np.arange(R), indexing="ij")
    for ky in range(R // 2 + 1):
        edge = ky in (0, R // 2)
        for kx in range(R // 2 + 1 if edge else R):
            angle = 2 * np.pi * ((kx * y + ky * x) % R) / R
            alone = edge and kx in (0, R // 2)
            pick = np.zeros((R, R // 2 + 1))
            pick[kx, ky] += 0.5
            pick[(-kx) % R if edge else kx, ky] += 0.5
            for part in (np.cos(angle),) if alone else (np.cos(angle), -np.sin(angle)):
                fwd.append(part)
                inv.append(part * (1 if alone else 2) / R**2)
                sel.append(pick.ravel())
    fwd, inv, sel = np.array(fwd), np.array(inv), np.array(sel)
    n = len(fwd)
    forward = np.zeros((R, 2, R, 2, n))
    inverse = np.zeros((2, n, R, 2, R))
    for p in range(2):
        forward[:, p, :, p, :] = fwd.transpose(1, 2, 0)
        inverse[p, :, :, p, :] = inv
    spread = np.concatenate([sel, sel], 0).T
    return (forward.reshape(P, P).astype(np.float32), inverse.reshape(P, P).astype(np.float32),
            np.ascontiguousarray(spread, np.float32))


def norm_coefficients(nc, ctx, block, name, partials, group_avg, psum, out):
    def sem(what):
        return ctx.enter_context(nc.semaphore(f"{name}_{what}"))

    step, avg_in, avg_out, dev_in, dev_out, root = (
        sem(w) for w in ("step", "avg_in", "avg_out", "dev_in", "dev_out", "root"))
    own = ctx.enter_context(nc.sbuf_tensor(f"{name}_own", [P, B, 2], F32))
    dev = ctx.enter_context(nc.sbuf_tensor(f"{name}_dev", [P, B], F32))
    var = ctx.enter_context(nc.sbuf_tensor(f"{name}_var", [P, B], F32))
    std = ctx.enter_context(nc.sbuf_tensor(f"{name}_std", [P, B], F32))
    tmp = ctx.enter_context(nc.sbuf_tensor(f"{name}_tmp", [P, B], F32))

    def vector(dve):
        count = [0]

        def then_wait(instruction):
            count[0] += 1
            instruction.then_inc(step, 1)
            dve.wait_ge(step, count[0])

        for b in range(B):
            then_wait(nc.vector.bn_aggr(own[:, b, :], partials[:, b, :]))
        dve.sem_inc(avg_in, 1)
        dve.wait_ge(avg_out, 1)
        then_wait(nc.vector.tensor_copy(out[:, :, 0], psum[:, 0:2 * B].rearrange("p (b s) -> p b s", b=B)[:, :, 0]))
        then_wait(nc.vector.tensor_copy(var[:], psum[:, 0:2 * B].rearrange("p (b s) -> p b s", b=B)[:, :, 1]))
        then_wait(nc.vector.tensor_tensor(tmp[:], own[:, :, 0], out[:, :, 0], ALU.subtract))
        then_wait(nc.vector.tensor_tensor(dev[:], tmp[:], tmp[:], ALU.mult))
        dve.sem_inc(dev_in, 1)
        dve.wait_ge(dev_out, 1)
        then_wait(nc.vector.tensor_tensor(tmp[:], var[:], psum[:, 8:8 + B], ALU.add))
        nc.vector.tensor_scalar(var[:], tmp[:], GN_EPS, None, ALU.add).then_inc(root, 1)
        dve.wait_ge(root, 2)
        then_wait(nc.vector.reciprocal(std[:], dev[:]))
        then_wait(nc.vector.tensor_tensor(tmp[:], std[:], std[:], ALU.mult))
        then_wait(nc.vector.tensor_tensor(dev[:], tmp[:], var[:], ALU.mult))
        then_wait(nc.vector.tensor_scalar(tmp[:], dev[:], -0.5, 1.5, ALU.mult, ALU.add))
        then_wait(nc.vector.tensor_tensor(out[:, :, 1], tmp[:], std[:], ALU.mult))

    def tensor(pe):
        pe.wait_ge(avg_in, 1)
        nc.tensor.matmul(psum[:, 0:2 * B], group_avg[:], own[:].rearrange("p b s -> p (b s)"),
                         start=True, stop=True).then_inc(avg_out, 1)
        pe.wait_ge(dev_in, 1)
        nc.tensor.matmul(psum[:, 8:8 + B], group_avg[:], dev[:], start=True, stop=True).then_inc(dev_out, 1)

    def scalar(act):
        act.wait_ge(root, 1)
        nc.scalar.activation(dev[:], var[:], ACT.Sqrt).then_inc(root, 1)

    return vector, tensor, scalar


def two_layers(nc, x, wqkv, wdw0, wproj, temperature, a1, a2, a3, a4, filt, win, wdw1, wout,
               identity_in, group_in, forward_in, inverse_in, spread_in, out):
    H = x.shape[2]
    C = H // R
    xv, ov = (a.rearrange("b (p t) h w -> b p t (h w)", t=T) for a in (x, out))
    v_d = nc.dram_tensor("v_scratch", [B, T, P, (H + R) * W], F32).ap()
    x1_d = nc.dram_tensor("x1_scratch", [B, P, T, H * W], F32).ap()
    gram_d = nc.dram_tensor("gram_scratch", [B, PAIRS, 2 * HC, 2 * HC], F32).ap()
    norm_d = nc.dram_tensor("norm_scratch", [B, KT * P], F32).ap()
    mix_d = nc.dram_tensor("mix_scratch", [B, CH, CH], F32).ap()

    with ExitStack() as whole:
        def keep(name, shape):
            return whole.enter_context(nc.sbuf_tensor(name, shape, F32))

        banks = whole.enter_context(nc.psum_tensor("banks", [P, 8, 512], F32))
        gn0, gn1 = keep("gn0", [P, B, 2]), keep("gn1", [P, B, 2])
        group_avg = keep("group_avg", [P, P])
        identity = keep("identity", [P, P])
        gram = keep("gram", [P, B, PAIRS * 2 * HC])
        squares = keep("squares", [P, B, KT, C + 1])

        with ExitStack() as ctx:
            def sb(name, shape):
                return ctx.enter_context(nc.sbuf_tensor(name, shape, F32))

            def sem(name):
                return ctx.enter_context(nc.semaphore(name))

            xs = sb("st_x", [P, 2, T, CW])
            partials = sb("st_partials", [P, B, C * T * 12])
            st_loaded = [sem("st_loaded0"), sem("st_loaded1")]
            consts_loaded, st_used, passed = sem("st_consts"), sem("st_used"), sem("st_passed")
            block = ctx.enter_context(nc.Block())
            vector, tensor, scalar = norm_coefficients(nc, ctx, block, "gn0", partials, group_avg,
                                                       banks[:, 0, :], gn0)

            @block.sync
            def _(sp):
                sp.dma_start(group_avg[:], group_in).then_inc(consts_loaded, 16)
                sp.dma_start(identity[:], identity_in).then_inc(consts_loaded, 16)
                for b in range(B):
                    def load(c, s):
                        after(sp, st_used, b * C + c - 1)
                        end_waits(sp, passed)
                        sp.dma_start(xs[:, s], xv[b][:, :, bass.ds(c * CW, CW)]).then_inc(st_loaded[s], 16)
                    over_chunks(sp, C, load)
                sp.wait_ge(consts_loaded, 32)

            @block.vector
            def _(dve):
                for b in range(B):
                    def stats(c, s):
                        dve.wait_ge(st_loaded[s], (c - s + b * C) * 8 + 16)
                        for t in range(T):
                            for h in range(2):
                                last = nc.vector.bn_stats(
                                    partials[:, b, bass.ds(c * (T * 12) + (t * 2 + h) * 6, 6)],
                                    xs[:, s, t, h * HALF:(h + 1) * HALF])
                        last.then_inc(st_used, 1)
                    over_chunks(dve, C, stats)
                dve.wait_ge(st_used, B * C)
                vector(dve)

            @block.tensor
            def _(pe):
                pe.wait_ge(consts_loaded, 32)
                tensor(pe)

            @block.scalar
            def _(act):
                scalar(act)

        with ExitStack() as ctx:
            def sb(name, shape, dtype=F32):
                return ctx.enter_context(nc.sbuf_tensor(name, shape, dtype))

            def sem(name):
                return ctx.enter_context(nc.semaphore(name))

            w_high, w_low = sb("wq_high", [P, T, 3 * CH], F32R), sb("wq_low", [P, T, 3 * CH], F32R)
            taps = sb("taps0", [P, QT, 9])
            xs = sb("a_x", [P, T, CW])
            x_high, x_low = sb("x_high", [P, 2, T, CW], F32R), sb("x_low", [P, 2, T, CW], F32R)
            u = sb("u", [P, RING, UR, UW])
            carry = sb("carry", [P, QT, 2, W])
            z = sb("z", [P, 3, 2, CW])
            y = sb("y", [P, RING, CW])
            junk = sb("junk", [P, CW])
            qkT = sb("qkT", [P, 2, R, CH])
            up = [banks[:, 2 * i:2 * i + 2, :].rearrange("p a n -> p (a n)") for i in range(2)]
            turned = banks[:, 4:6, :].rearrange("p a n -> p (a n)")
            gram_ps = banks[0:2 * HC, 6, 0:PAIRS * 2 * HC]

            weights_loaded, split = sem("a_weights"), sem("a_split")
            x_loaded = sem("a_x_loaded")
            passed = sem("a_passed")
            cleared = sem("a_cleared")
            normalised = sem("a_normalised")
            xn_ready = sem("a_xn")
            up_ready = sem("a_up")
            u_written = sem("a_u")
            carried_out = sem("a_carried_out")
            carried_in = sem("a_carried_in")
            products = sem("a_products")
            added = sem("a_added")
            early_taps = sem("a_early_taps")
            late_taps = sem("a_late_taps")
            cut = sem("a_cut")
            y_ready = sem("a_y")
            squared = sem("a_squared")
            turned_ready = sem("a_turned")
            turned_kept = sem("a_turned_kept")
            gram_ready = sem("a_gram")
            gram_added = sem("a_gram_added")
            v_stored = [sem(f"a_v{i}") for i in range(T)]
            block = ctx.enter_context(nc.Block())

            NC = C + 1
            CHAIN = len(DVE_TAPS)
            EARLY = CHAIN // 2

            def shifted(t, tap, rows):
                dy, dx = tap // 3, tap % 3
                return u[:, t % RING, dy:dy + rows, dx:dx + W]

            def image(ap, rows):
                return ap[:, 0:rows * W].rearrange("p (r w) -> p r w", w=W)

            def wait_slot_read(engine, g, t):
                before = max(k for k in range(-QT, t) if k % QT % RING == t % RING)
                g, tile = (g, before) if before >= 0 else (g - 1, before + QT)
                if tile < KT:
                    after(engine, turned_ready, g * KT + tile + 1)
                    after(engine, squared, g * KT + tile + 1)
                else:
                    after(engine, v_stored[tile - KT], (g + 1) * 16)

            @block.sync
            def _(sp):
                raw = z[:].rearrange("p a b n -> p (a b n)")[:, 0:T * 3 * CH].rearrange("p (t o) -> p t o", t=T)
                sp.dma_start(raw, wqkv.rearrange("(p t) o -> p t o", t=T)).then_inc(weights_loaded, 16)
                sp.dma_start(taps[:], wdw0.rearrange("(t p) k -> p t k", p=P)).then_inc(weights_loaded, 16)

                def load(b, c):
                    after(sp, xn_ready, (b * C + c) * T)
                    end_waits(sp, passed)
                    sp.dma_start(xs[:], xv[b][:, :, bass.ds(c * CW, CW)]).then_inc(x_loaded, 16)

                def store_v(b, c, rows):
                    for t in range(KT, QT):
                        sp.wait_ge(y_ready, (b * NC + c) * QT + t + 1)
                        end_waits(sp, passed)
                        sp.dma_start(v_d[b, t - KT][:, bass.ds(c * CW, rows * W)],
                                     y[:, t % RING, 0:rows * W]).then_inc(v_stored[t - KT], 16)

                load(0, 0)
                for b in range(B):
                    def chunk(c, s):
                        if not (isinstance(c, int) and c == C - 1):
                            load(b, c + 1)
                        elif b + 1 < B:
                            load(b + 1, 0)
                        store_v(b, c, R)
                    over_chunks(sp, C, chunk)
                    store_v(b, C, 1)
                for t in range(T):
                    sp.wait_ge(v_stored[t], B * NC * 16)

            @block.tensor
            def _(pe):
                pe.wait_ge(split, 2)
                for b in range(B):
                    def turn(c, t, rows):
                        g = b * NC + c
                        pe.wait_ge(y_ready, g * QT + t + 1)
                        after(pe, turned_kept, g * KT + t)
                        for i in range(rows):
                            last = nc.tensor.transpose(turned[:, i * P:(i + 1) * P],
                                                       y[:, t % RING, i * W:(i + 1) * W], identity[:])
                        last.then_inc(turned_ready, 1)

                    def multiply_gram(c, rows):
                        g = b * NC + c
                        pe.wait_ge(turned_kept, (g + 1) * KT)
                        after(pe, gram_added, g)
                        for p in range(PAIRS):
                            pair = slice(p * 2 * HC, (p + 1) * 2 * HC)
                            for i in range(rows):
                                last = nc.tensor.matmul(gram_ps[:, pair], qkT[:, 0, i, pair], qkT[:, 1, i, pair],
                                                        start=(i == 0), stop=(i == rows - 1))
                        last.then_inc(gram_ready, 1)

                    def chunk(c, s):
                        first = isinstance(c, int) and c == 0
                        pe.wait_ge(xn_ready, (b * C + c + 1) * T)
                        for t in range(QT):
                            m = (b * C + c) * QT + t
                            after(pe, carried_out, m - 1)
                            for h in range(2):
                                to = up[(s * QT + t) % 2][:, h * HALF:(h + 1) * HALF]
                                for k in range(T):
                                    for i, (w, xp) in enumerate(((w_high, x_high), (w_low, x_high), (w_high, x_low))):
                                        last = nc.tensor.matmul(
                                            to, w[:, k, t * P:(t + 1) * P], xp[:, s, k, h * HALF:(h + 1) * HALF],
                                            start=(k == 0 and i == 0), stop=(k == T - 1 and i == 2))
                            last.then_inc(up_ready, 1)
                            if t >= LAG:
                                turn(c, t - LAG, R)
                            elif QT - LAG + t < KT and not first:
                                turn(c - 1, QT - LAG + t, R)
                            elif t == KT - QT + LAG and not first:
                                multiply_gram(c - 1, R)
                    over_chunks(pe, C, chunk)
                    for t in range(QT - LAG, KT):
                        turn(C - 1, t, R)
                    multiply_gram(C - 1, R)
                    for t in range(KT):
                        turn(C, t, 1)
                    multiply_gram(C, 1)

            @block.scalar
            def _(act):
                act.wait_ge(weights_loaded, 32)
                act.wait_ge(cleared, 2)
                for b in range(B):
                    def keep(c, t, rows):
                        g = b * NC + c
                        act.wait_ge(turned_ready, g * KT + t + 1)
                        after(act, gram_ready, g)
                        nc.scalar.copy(qkT[:, t // T, 0:rows, t % T * P:(t % T + 1) * P],
                                       turned[:, 0:rows * P].rearrange("p (r d) -> p r d", d=P)).then_inc(turned_kept, 1)

                    def square(c, t, rows):
                        q = (b * NC + c) * KT + t
                        act.wait_ge(y_ready, (b * NC + c) * QT + t + 1)
                        after(act, squared, q)
                        nc.scalar.activation(junk[:, 0:rows * W], y[:, t % RING, 0:rows * W], ACT.Square,
                                             accum_out=squares[:, b, t, bass.ds(c, 1)]).then_inc(squared, 1)

                    def multiply(c, t, rows):
                        g = b * NC + c
                        n = g * QT + t
                        act.wait_ge(u_written, n + 1)
                        act.wait_ge(carried_in, n + 1)
                        wait_slot_read(act, g, t)
                        after(act, added, 2 * (n - 2))
                        for k, tap in enumerate(ACT_TAPS):
                            to = y[:, t % RING, :] if k == 0 else z[:, t % 3, k - 1, :]
                            nc.scalar.activation(image(to, rows), shifted(t, tap, rows), ACT.Copy,
                                                 scale=taps[:, t, tap:tap + 1]).then_inc(products, 1)

                    def chunk(c, s):
                        first = isinstance(c, int) and c == 0
                        for t in range(QT):
                            g = b * NC + c
                            n = g * QT + t
                            m = (b * C + c) * QT + t
                            act.wait_ge(up_ready, m + 1)
                            after(act, y_ready, n - LAG + 1)
                            rows_in = up[(s * QT + t) % 2].rearrange("p (r w) -> p r w", w=W)
                            nc.scalar.copy(u[:, t % RING, 2:UR, 1:1 + W], rows_in).then_inc(u_written, 1)
                            act.wait_ge(carried_in, n + 1)
                            nc.scalar.copy(carry[:, t, :, :], rows_in[:, R - 2:R, :]).then_inc(carried_out, 1)
                            if t > LAG:
                                keep(c, t - LAG - 1, R)
                            elif QT - LAG + t - 1 < KT and not first:
                                keep(c - 1, QT - LAG + t - 1, R)
                            if t >= LAG:
                                square(c, t - LAG, R)
                            elif QT + t - LAG < KT and not first:
                                square(c - 1, QT + t - LAG, R)
                            multiply(c, t, R)
                    over_chunks(act, C, chunk)
                    for t in range(QT):
                        if t < KT + LAG - QT:
                            square(C - 1, QT + t - LAG, R)
                        if t == 0:
                            for i in range(QT - LAG - 1, KT):
                                keep(C - 1, i, R)
                        multiply(C, t, 1)
                        if 3 <= t < KT + 3:
                            square(C, t - 3, 1)
                            keep(C, t - 3, 1)

            @block.gpsimd
            def _(pool):
                nc.gpsimd.memset(u[:], 0.0).then_inc(cleared, 1)
                nc.gpsimd.memset(gram[:], 0.0).then_inc(cleared, 1)
                pool.wait_ge(cleared, 2)

                def carry_in(b, c, t):
                    n = (b * NC + c) * QT + t
                    after(pool, y_ready, n - LAG + 1)
                    top = u[:, t % RING, 0:2, 1:1 + W]
                    if isinstance(c, int) and c == 0:
                        nc.gpsimd.memset(top, 0.0).then_inc(carried_in, 1)
                        return
                    pool.wait_ge(carried_out, (b * C + c - 1) * QT + t + 1)
                    if isinstance(c, int) and c == C:
                        pool.wait_ge(u_written, n)
                        nc.gpsimd.memset(u[:, t % RING, 2, 1:1 + W], 0.0).then_inc(u_written, 1)
                    end_waits(pool, passed)
                    nc.gpsimd.tensor_copy(top, carry[:, t, :, :]).then_inc(carried_in, 1)

                def split_low(i, s, k):
                    pool.wait_ge(normalised, 2 * i + 2)
                    after(pool, up_ready, (i - 1) * QT)
                    nc.gpsimd.tensor_tensor(x_low[:, s, k], xs[:, k], x_high[:, s, k].bitcast(F32),
                                            ALU.subtract).then_inc(xn_ready, 1)

                for k in range(T):
                    split_low(0, 0, k)
                carry_in(0, 0, 0)
                for b in range(B):
                    def steps(c, s, rows):
                        fixed = isinstance(c, int)
                        for t in range(QT):
                            n = (b * NC + c) * QT + t
                            if t + 1 < QT:
                                carry_in(b, c, t + 1)
                            elif not (fixed and c == C):
                                carry_in(b, c + 1, 0)
                            elif b + 1 < B:
                                carry_in(b + 1, 0, 0)
                            pool.wait_ge(products, 3 * n + 3)
                            to = y[:, t % RING, 0:rows * W]
                            for k in range(2):
                                nc.gpsimd.tensor_tensor(to, to, z[:, t % 3, k, 0:rows * W], ALU.add).then_inc(added, 1)
                                pool.wait_ge(added, 2 * n + k + 1)
                            if t in (3, 4, 5):
                                if not (fixed and c >= C - 1):
                                    split_low(b * C + c + 1, 1 - s, t - 3)
                                elif c == C and b + 1 < B:
                                    split_low((b + 1) * C, 0, t - 3)

                    over_chunks(pool, C, lambda c, s: steps(c, s, R))
                    steps(C, 0, 1)

            @block.vector
            def _(dve):
                dve.wait_ge(weights_loaded, 32)
                raw = z[:].rearrange("p a b n -> p (a b n)")[:, 0:T * 3 * CH].rearrange("p (t o) -> p t o", t=T)
                nc.vector.tensor_copy(w_high[:], raw).then_inc(split, 1)
                dve.wait_ge(split, 1)
                nc.vector.tensor_tensor(w_low[:], raw, w_high[:].bitcast(F32), ALU.subtract).then_inc(split, 1)
                dve.wait_ge(cleared, 2)

                def normalise(b, c, s):
                    i = b * C + c
                    dve.wait_ge(x_loaded, 16 * (i + 1))
                    after(dve, up_ready, (i - 1) * QT)
                    for to in (x_high[:, s], xs[:]):
                        nc.vector.tensor_scalar(to, xs[:], gn0[:, b, 0:1], gn0[:, b, 1:2],
                                                ALU.subtract, ALU.mult).then_inc(normalised, 1)

                def add_gram(b, c):
                    dve.wait_ge(gram_ready, b * NC + c + 1)
                    after(dve, gram_added, b * NC + c)
                    total = gram[0:2 * HC, b, :]
                    nc.vector.tensor_tensor(total, total, gram_ps, ALU.add).then_inc(gram_added, 1)

                def add_tap(b, c, t, k, rows):
                    n = (b * NC + c) * QT + t
                    if k == 0:
                        dve.wait_ge(added, 2 * n + 2)
                    elif k <= EARLY:
                        dve.wait_ge(early_taps, n * EARLY + k)
                    else:
                        dve.wait_ge(late_taps, n * (CHAIN - EARLY - 1) + k - EARLY)
                    done = (early_taps if k < EARLY else late_taps if k < CHAIN - 1
                            else cut if isinstance(c, int) and c == 0 else y_ready)
                    to = image(y[:, t % RING, :], rows)
                    tap = DVE_TAPS[k]
                    nc.vector.scalar_tensor_tensor(to, shifted(t, tap, rows), taps[:, t, tap:tap + 1], to,
                                                   ALU.mult, ALU.add).then_inc(done, 1)

                normalise(0, 0, 0)
                for k in range(EARLY):
                    add_tap(0, 0, 0, k, R)
                for b in range(B):
                    def steps(c, s, rows):
                        fixed = isinstance(c, int)
                        for t in range(QT):
                            if t + 1 < QT:
                                following = (b, c, t + 1, rows)
                            elif not (fixed and c == C):
                                following = (b, c + 1, 0, 1 if fixed and c + 1 == C else R)
                            else:
                                following = (b + 1, 0, 0, R) if b + 1 < B else None
                            for k in range(EARLY, CHAIN):
                                add_tap(b, c, t, k, rows)
                                if following:
                                    fb, fc, ft, frows = following
                                    add_tap(fb, fc, ft, k - EARLY, frows)
                            to = image(y[:, t % RING, :], rows)
                            if fixed and c == 0:
                                dve.wait_ge(cut, b * QT + t + 1)
                                nc.vector.memset(to[:, 0, :], 0.0).then_inc(y_ready, 1)
                            if t == 5 and not (fixed and c == 0):
                                add_gram(b, c - 1)
                            if t == 1:
                                if not (fixed and c >= C - 1):
                                    normalise(b, c + 1, 1 - s)
                                elif c == C and b + 1 < B:
                                    normalise(b + 1, 0, 0)

                    over_chunks(dve, C, lambda c, s: steps(c, s, R))
                    steps(C, 0, 1)
                    add_gram(b, C)

        with ExitStack() as ctx:
            def sb(name, shape):
                return ctx.enter_context(nc.sbuf_tensor(name, shape, F32))

            def sem(name):
                return ctx.enter_context(nc.semaphore(name))

            NB = B * PAIRS
            K4 = len(TOPK)
            ssq, rn, nt0, nt1 = (sb(n, [P, B * KT]) for n in ("ssq", "rn", "nt0", "nt1"))
            qn = sb("qn", [P, B, PAIRS])
            kn = sb("kn", [P, B, PAIRS, HC])
            temp = sb("temp", [P, PAIRS])
            gains = sb("gains", [P, K4])
            qk = sb("qk", [P, NB, HC])
            scaled = sb("scaled", [P, NB, HC])
            logits = sb("logits", [P, NB, HC])
            left = sb("left", [P, NB, HC])
            tops = sb("tops", [P, NB, 40])
            lowered = sb("lowered", [P, NB])
            expd = sb("expd", [P, NB, HC])
            masked = sb("masked", [P, K4, NB, HC])
            sums = sb("sums", [P, K4, NB])
            shares = sb("shares", [P, K4, NB])
            mixed = sb("mixed", [P, NB, HC])
            diag = sb("diag", [P, NB, P])
            wp = sb("wp", [P, PAIRS, CH])
            mt = sb("mt", [P, NB, CH])
            t_moved = sem("t_moved")
            t_loaded, t_norm, t_back = sem("t_loaded"), sem("t_norm"), sem("t_back")
            t_zeroed, t_chain, t_root = sem("t_zeroed"), sem("t_chain"), sem("t_root")
            t_exp, t_diag, t_mt, t_mt_kept, t_stored = (
                sem(n) for n in ("t_exp", "t_diag", "t_mt", "t_mt_kept", "t_stored"))
            block = ctx.enter_context(nc.Block())

            @block.sync
            def _(sp):
                with nc.allow_non_contiguous_dma(reason="tables of a few hundred numbers"):
                    wpv = wproj.rearrange("(p s i) o -> s i p o", s=2, i=HC)
                    tv = temperature.rearrange("(p s) a b -> s (a b) p", s=2)
                    sp.wait_ge(t_zeroed, 1)
                    for s in range(2):
                        sp.dma_start(wp[s * SLOT:s * SLOT + HC], wpv[s]).then_inc(t_loaded, 16)
                        sp.dma_start(temp[s * SLOT:(s + 1) * SLOT], tv[s].to_broadcast([SLOT, PAIRS])).then_inc(t_loaded, 16)
                    for i, a in enumerate((a1, a2, a3, a4)):
                        sp.dma_start(gains[:, i:i + 1], a.rearrange("(a b) -> a b", a=1).to_broadcast([P, 1])).then_inc(t_loaded, 16)
                    for b in range(B):
                        sp.dma_start(gram_d[b].rearrange("r i j -> i r j"),
                                     gram[0:2 * HC, b, :].rearrange("p (r j) -> p r j", r=PAIRS)).then_inc(t_moved, 16)
                    sp.wait_ge(t_norm, 1)
                    for b in range(B):
                        sp.dma_start(norm_d[b].rearrange("(t p) -> p t", p=P), rn[:, b * KT:(b + 1) * KT]).then_inc(t_back, 16)
                    sp.wait_ge(t_back, 16 * B)
                    sp.wait_ge(t_moved, 16 * B)
                    for n in range(NB):
                        for s in range(2):
                            own = slice(s * HC, (s + 1) * HC)
                            sp.dma_start(qk[s * SLOT:s * SLOT + HC, n, :], gram_d[n // PAIRS, n % PAIRS][own, own]
                                         ).then_inc(t_moved, 16)
                    for b in range(B):
                        nq = norm_d[b, 0:CH].rearrange("(p s i) -> s i p", s=2, i=HC)
                        nk = norm_d[b, CH:2 * CH].rearrange("(a p s i) -> s a p i", a=1, s=2, i=HC)
                        for s in range(2):
                            sp.dma_start(qn[s * SLOT:s * SLOT + HC, b, :], nq[s]).then_inc(t_back, 16)
                            sp.dma_start(kn[s * SLOT:(s + 1) * SLOT, b], nk[s].to_broadcast([SLOT, PAIRS, HC])).then_inc(t_back, 16)
                for n in range(NB):
                    b, p = n // PAIRS, n % PAIRS
                    sp.wait_ge(t_mt_kept, n + 1)
                    for s in range(2):
                        row = (2 * p + s) * HC
                        sp.dma_start(mix_d[b, row:row + HC, :], mt[s * SLOT:s * SLOT + HC, n, :]).then_inc(t_stored, 16)
                sp.wait_ge(t_stored, 16 * 2 * NB)

            @block.scalar
            def _(act):
                act.wait_ge(t_root, 1)
                nc.scalar.activation(nt0[:], ssq[:], ACT.Sqrt).then_inc(t_root, 1)
                act.wait_ge(t_exp, 1)
                for n in range(NB):
                    last = nc.scalar.activation(expd[:, n, :], logits[:, n, :], ACT.Exp, bias=lowered[:, n:n + 1])
                last.then_inc(t_exp, 1)
                for n in range(NB):
                    act.wait_ge(t_mt, n + 1)
                    nc.scalar.copy(mt[:, n, :], banks[:, n, 0:CH]).then_inc(t_mt_kept, 1)

            @block.tensor
            def _(pe):
                pe.wait_ge(t_diag, 1)
                pe.wait_ge(t_loaded, 16 * 8)
                for n in range(NB):
                    nc.tensor.matmul(banks[:, n, 0:CH], diag[:, n, :], wp[:, n % PAIRS, :],
                                     start=True, stop=True).then_inc(t_mt, 1)

            @block.vector
            def _(dve):
                count = [0]

                def then_wait(instruction):
                    count[0] += 1
                    instruction.then_inc(t_chain, 1)
                    dve.wait_ge(t_chain, count[0])

                def settle(instructions):
                    for i in instructions:
                        i.then_inc(t_chain, 1)
                        count[0] += 1
                    dve.wait_ge(t_chain, count[0])

                settle([nc.vector.memset(a[:], 0.0) for a in (wp, qn, qk, diag)])
                dve.sem_inc(t_zeroed, 1)
                then_wait(nc.vector.reduce_sum(rn[:], squares[:].rearrange("p b t c -> p (b t) c"), AX_X))
                nc.vector.tensor_scalar(ssq[:], rn[:], 1e-24, None, ALU.max).then_inc(t_root, 1)
                dve.wait_ge(t_root, 2)
                then_wait(nc.vector.reciprocal(nt1[:], nt0[:]))
                then_wait(nc.vector.tensor_tensor(nt0[:], nt1[:], nt1[:], ALU.mult))
                then_wait(nc.vector.tensor_tensor(rn[:], nt0[:], ssq[:], ALU.mult))
                then_wait(nc.vector.tensor_scalar(nt0[:], rn[:], -0.5, 1.5, ALU.mult, ALU.add))
                nc.vector.tensor_tensor(rn[:], nt0[:], nt1[:], ALU.mult).then_inc(t_norm, 1)
                dve.wait_ge(t_loaded, 16 * 8)
                dve.wait_ge(t_back, 16 * 5 * B)
                knv = kn[:].rearrange("p b r d -> p (b r) d")
                dve.wait_ge(t_moved, 16 * (B + 2 * NB))
                then_wait(nc.vector.tensor_tensor(scaled[:], qk[:], knv, ALU.mult))
                settle([nc.vector.tensor_scalar(logits[:, n, :], scaled[:, n, :], qn[:, n // PAIRS, n % PAIRS:n % PAIRS + 1],
                                                temp[:, n % PAIRS:n % PAIRS + 1], ALU.mult, ALU.mult) for n in range(NB)])
                for e in range(5):
                    now = logits if e == 0 else left
                    settle([nc.vector.max(tops[:, n, 8 * e:8 * e + 8], now[:, n, :]) for n in range(NB)])
                    if e < 4:
                        settle([nc.vector.match_replace(left[:, n, :], tops[:, n, 8 * e:8 * e + 8], now[:, n, :], LOWEST)
                                for n in range(NB)])
                nc.vector.tensor_scalar(lowered[:], tops[:, :, 0], -1.0, None, ALU.mult).then_inc(t_exp, 1)
                dve.wait_ge(t_exp, 2)
                settle([nc.vector.scalar_tensor_tensor(masked[:, i, n, :], logits[:, n, :], tops[:, n, k - 1:k],
                                                       expd[:, n, :], ALU.is_ge, ALU.mult)
                        for i, k in enumerate(TOPK) for n in range(NB)])
                then_wait(nc.vector.reduce_sum(sums[:].rearrange("p a n -> p (a n)"),
                                               masked[:].rearrange("p a n d -> p (a n) d"), AX_X))
                then_wait(nc.vector.reciprocal(shares[:], sums[:]))
                settle([nc.vector.tensor_scalar(sums[:, i, :], shares[:, i, :], gains[:, i:i + 1], None, ALU.mult)
                        for i in range(K4)])
                settle([nc.vector.tensor_scalar(mixed[:, n, :], masked[:, 0, n, :], sums[:, 0, n:n + 1], None, ALU.mult)
                        for n in range(NB)])
                for i in range(1, K4):
                    settle([nc.vector.scalar_tensor_tensor(mixed[:, n, :], masked[:, i, n, :], sums[:, i, n:n + 1],
                                                           mixed[:, n, :], ALU.mult, ALU.add) for n in range(NB)])
                settle([nc.vector.tensor_copy(diag[s * SLOT:s * SLOT + HC, :, s * SLOT:s * SLOT + HC],
                                              mixed[s * SLOT:s * SLOT + HC]) for s in range(2)])
                dve.sem_inc(t_diag, 1)

        with ExitStack() as ctx:
            def sb(name, shape):
                return ctx.enter_context(nc.sbuf_tensor(name, shape, F32))

            def sem(name):
                return ctx.enter_context(nc.semaphore(name))

            mix = sb("mix", [P, B, T, CH])
            vs = sb("vs", [P, 2, T, CW])
            xs = sb("p_x", [P, 2, T, CW])
            partials = sb("p_partials", [P, B, C * T * 12])
            up = [banks[:, 2 * i:2 * i + 2, :].rearrange("p a n -> p (a n)") for i in range(2)]
            mix_loaded, passed = sem("p_mix"), sem("p_passed")
            v_loaded, x_loaded, x1_stored = ([sem(f"p_{n}{i}") for i in range(2)] for n in ("v", "x", "x1"))
            mixed_ready = sem("p_mixed")
            x1_ready = sem("p_x1_ready")
            counted = sem("p_counted")
            block = ctx.enter_context(nc.Block())
            vector, tensor, scalar = norm_coefficients(nc, ctx, block, "gn1", partials, group_avg,
                                                       banks[:, 7, :], gn1)

            @block.sync
            def _(sp):
                for b in range(B):
                    sp.dma_start(mix[:, b], mix_d[b].rearrange("(k p) o -> p k o", p=P)).then_inc(mix_loaded, 16)
                for b in range(B):
                    def load(c, s):
                        i = b * C + c
                        after(sp, mixed_ready, (i - 1) * T)
                        end_waits(sp, passed)
                        sp.dma_start(vs[:, s], v_d[b].rearrange("t p n -> p t n")[:, :, bass.ds(c * CW + W, CW)]
                                     ).then_inc(v_loaded[s], 16)
                        after(sp, counted, (i - 1) * T)
                        end_waits(sp, passed)
                        after(sp, x1_stored[s], (b * C + c - s) * 8)
                        end_waits(sp, passed)
                        sp.dma_start(xs[:, s], xv[b][:, :, bass.ds(c * CW, CW)]).then_inc(x_loaded[s], 16)
                    over_chunks(sp, C, load)

            @block.tensor
            def _(pe):
                pe.wait_ge(mix_loaded, 16 * B)
                for b in range(B):
                    def chunk(c, s):
                        pe.wait_ge(v_loaded[s], (b * C + c - s) * 8 + 16)
                        for m in range(T):
                            i = (b * C + c) * T + m
                            after(pe, x1_ready, i - 1)
                            for h in range(2):
                                for k in range(T):
                                    last = nc.tensor.matmul(
                                        up[(s * T + m) % 2][:, h * HALF:(h + 1) * HALF],
                                        mix[:, b, k, m * P:(m + 1) * P], vs[:, s, k, h * HALF:(h + 1) * HALF],
                                        start=(k == 0), stop=(k == T - 1))
                            last.then_inc(mixed_ready, 1)
                    over_chunks(pe, C, chunk)
                tensor(pe)

            @block.scalar
            def _(act):
                for b in range(B):
                    def store(c, s):
                        act.wait_ge(x1_ready, (b * C + c + 1) * T)
                        end_waits(act, passed)
                        act.dma_start(x1_d[b][:, :, bass.ds(c * CW, CW)], xs[:, s]).then_inc(x1_stored[s], 16)
                    over_chunks(act, C, store)
                for s in range(2):
                    act.wait_ge(x1_stored[s], B * C * 8)
                scalar(act)

            @block.vector
            def _(dve):
                for b in range(B):
                    def chunk(c, s):
                        dve.wait_ge(x_loaded[s], (b * C + c - s) * 8 + 16)
                        for m in range(T):
                            i = (b * C + c) * T + m
                            dve.wait_ge(mixed_ready, i + 1)
                            nc.vector.tensor_tensor(xs[:, s, m, :], up[(s * T + m) % 2], xs[:, s, m, :],
                                                    ALU.add).then_inc(x1_ready, 1)
                            dve.wait_ge(x1_ready, i + 1)
                            for h in range(2):
                                last = nc.vector.bn_stats(
                                    partials[:, b, bass.ds(c * (T * 12) + (m * 2 + h) * 6, 6)],
                                    xs[:, s, m, h * HALF:(h + 1) * HALF])
                            last.then_inc(counted, 1)
                    over_chunks(dve, C, chunk)
                dve.wait_ge(counted, B * C * T)
                vector(dve)

        with ExitStack() as ctx:
            def sb(name, shape):
                return ctx.enter_context(nc.sbuf_tensor(name, shape, F32))

            def sem(name):
                return ctx.enter_context(nc.semaphore(name))

            NC = C + 1
            H2 = CH // 2
            REST = H2 - P
            wi = sb("wi", [P, T, CH])
            wo = sb("wo", [P, 2, CH])
            taps = sb("taps1", [P, T, 9])
            forward, inverse = sb("forward", [P, P]), sb("inverse", [P, P])
            half_filter = sb("half_filter", [R * (R // 2 + 1), CH])
            spread = sb("spread", [R * (R // 2 + 1), P])
            filt_sb = sb("filt_sb", [P, CH])
            xw = sb("f_xw", [P, 2, T, CW])
            xn = sb("f_xn", [P, 2, T, CW])
            xr = sb("f_xr", [P, 2, T, CW])
            pixels = sb("pixels", [P, 2, CH])
            spectra = sb("spectra", [P, 2, CH])
            u = sb("f_u", [P, 2, T, UR, UW])
            z = sb("f_z", [P, T, 2, CW])
            y = sb("f_y", [P, 2, T, CW])
            aside = sb("aside", [REST, CW])

            f_weights, filter_ready, f_cleared = sem("f_weights"), sem("f_filter"), sem("f_cleared")
            passed = sem("f_passed")
            x_loaded = [sem("f_x0"), sem("f_x1")]
            r_loaded = [sem("f_r0"), sem("f_r1")]
            o_stored = [sem("f_o0"), sem("f_o1")]
            xn_ready = sem("f_xn_ready")
            s1_ready = sem("f_s1")
            pixels_kept = sem("f_pixels")
            coef_ready = sem("f_coef")
            filtered = sem("f_filtered")
            inv_ready = sem("f_inv")
            u_written = sem("f_u_written")
            window_ready = sem("f_window")
            products = sem("f_products")
            added = sem("f_added")
            early_taps = sem("f_early_taps")
            late_taps = sem("f_late_taps")
            y_ready = sem("f_y_ready")
            gelu_done = sem("f_gelu")
            gated = sem("f_gated")
            out_ready = sem("f_out")
            summed = sem("f_summed")
            block = ctx.enter_context(nc.Block())
            CHAIN = len(DVE_TAPS)
            EARLY = CHAIN // 2
            s1_ps = [banks[:, i, 0:CH] for i in (0, 1)]
            coef_ps = [banks[:, i, 0:CH] for i in (2, 3)]
            inv_ps = [banks[:, i, 0:CH] for i in (4, 5)]
            OUTS = 2 * T
            OUT_AT, OUT_LATE = {5: [0], 6: [1], 7: [2]}, {0: [3], 1: [4, 5]}
            SUM_AT, SUM_LATE = {6: [0], 7: [1]}, {0: [2], 1: [3], 2: [4], 3: [5]}

            def shifted(t, s, tap, rows):
                dy, dx = tap // 3, tap % 3
                return u[:, s, t, dy:dy + rows, dx:dx + W]

            def rows_of(ap, rows):
                return ap[:, 0:rows * W].rearrange("p (r w) -> p r w", w=W)

            def over_slots(engine, body):
                over_chunks(engine, C, body, alone=2)
                for k in range(C, C + 4):
                    body(k, k % 2)

            def alive(k, chunk, end):
                return not isinstance(k, int) or 0 <= chunk < end

            def block_of(k, j):
                return alive(k, k if j >= 0 else k - 1, C)

            def stored(b, i, c=0, s=0):
                return (b * (C // 2 + (1 - i)) * 16) + (c - s) * 8

            def height(k, chunk):
                return 1 if isinstance(k, int) and chunk == C else R

            @block.sync
            def _(sp):
                loads = [(wi[:], win.rearrange("(p t) o -> p t o", t=T)), (wo[:, 0, :], wout[0:P]),
                         (wo[0:REST, 1, :], wout[P:H2]), (taps[:], wdw1.rearrange("(t p) k -> p t k", p=P)),
                         (forward[:], forward_in), (inverse[:], inverse_in),
                         (half_filter[:], filt), (spread[:], spread_in)]
                for to, source in loads:
                    sp.dma_start(to, source).then_inc(f_weights, 16)
                sp.wait_ge(f_cleared, 2)

                def load(b, c, s):
                    after(sp, xn_ready, (b * C + c - 1) * T)
                    end_waits(sp, passed)
                    sp.dma_start(xw[:, s], x1_d[b][:, :, bass.ds(c * CW, CW)]).then_inc(x_loaded[s], 16)

                load(0, 0, 0)
                for b in range(B):
                    def slot(k, s):
                        if alive(k, k + 1, C):
                            load(b, k + 1, 1 - s)
                        elif isinstance(k, int) and k == C and b + 1 < B:
                            load(b + 1, 0, 0)
                        if alive(k, k - 3, NC):
                            rows = height(k, k - 3)
                            sp.wait_ge(summed, (b * NC + k - 2) * OUTS)
                            end_waits(sp, passed)
                            if isinstance(k, int) and k == 3:
                                sp.dma_start(ov[b][:, :, 0:CW - W], xr[:, 1 - s, :, W:]).then_inc(o_stored[1 - s], 16)
                            else:
                                sp.dma_start(ov[b][:, :, bass.ds((k - 3) * CW - W, rows * W)],
                                             xr[:, 1 - s, :, 0:rows * W]).then_inc(o_stored[1 - s], 16)
                        if alive(k, k - 1, NC):
                            rows = height(k, k - 1)
                            after(sp, o_stored[1 - s], stored(b, 1 - s, k - 1, 1 - s))
                            end_waits(sp, passed)
                            if isinstance(k, int) and k == 1:
                                sp.dma_start(xr[:, 1 - s, :, W:], x1_d[b][:, :, 0:CW - W]).then_inc(r_loaded[1 - s], 16)
                            else:
                                sp.dma_start(xr[:, 1 - s, :, 0:rows * W],
                                             x1_d[b][:, :, bass.ds((k - 1) * CW - W, rows * W)]).then_inc(r_loaded[1 - s], 16)
                    over_slots(sp, slot)
                for i in range(2):
                    sp.wait_ge(o_stored[i], stored(B, i))

            @block.tensor
            def _(pe):
                pe.wait_ge(f_weights, 16 * 8)
                nc.tensor.matmul(banks[:, 7, 0:CH], spread[:], half_filter[:], start=True, stop=True).then_inc(filter_ready, 1)
                pe.wait_ge(filter_ready, 2)
                for b in range(B):
                    def slot(k, s):
                        if alive(k, k, C):
                            pe.wait_ge(xn_ready, (b * C + k + 1) * T)
                        for j in range(NBLK):
                            q = (b * C + k) * NBLK + j
                            if block_of(k, j):
                                after(pe, pixels_kept, q - 1)
                                for t in range(T):
                                    last = nc.tensor.matmul(s1_ps[j % 2], xn[:, s, t, j * P:(j + 1) * P], wi[:, t, :],
                                                            start=(t == 0), stop=(t == T - 1))
                                last.then_inc(s1_ready, 1)
                            if block_of(k, j - 1):
                                pe.wait_ge(pixels_kept, q)
                                after(pe, filtered, q - 2)
                                nc.tensor.matmul(coef_ps[(j - 1) % 2], forward[:], pixels[:, (j - 1) % 2, :],
                                                 start=True, stop=True).then_inc(coef_ready, 1)
                            if block_of(k, j - 2):
                                pe.wait_ge(filtered, q - 1)
                                after(pe, u_written, q - 3)
                                for t in range(T):
                                    last = nc.tensor.matmul(
                                        inv_ps[j % 2][:, t * P:(t + 1) * P], spectra[:, j % 2, t * P:(t + 1) * P],
                                        inverse[:], start=True, stop=True)
                                last.then_inc(inv_ready, 1)
                            for chunk, at, halves in ((k - 2, s, OUT_AT.get(j, [])), (k - 3, 1 - s, OUT_LATE.get(j, []))):
                                for w in halves if alive(k, chunk, NC) else []:
                                    g = b * NC + chunk
                                    m, h = w // 2, w % 2
                                    n = HALF if height(k, chunk) == R else W
                                    from_ = 0 if n == W else h * HALF
                                    if w == 0:
                                        pe.wait_ge(gated, g + 1)
                                    after(pe, summed, g * OUTS + w - 1)
                                    to = banks[:, 6 + w % 2, 0:n]
                                    nc.tensor.matmul(to, wo[:, 0, m * P:(m + 1) * P], y[:, at, 0, from_:from_ + n],
                                                     start=True, stop=False)
                                    nc.tensor.matmul(to, wo[0:REST, 1, m * P:(m + 1) * P], y[0:REST, at, 2, from_:from_ + n],
                                                     start=False, stop=True).then_inc(out_ready, 1)
                    over_slots(pe, slot)

            @block.scalar
            def _(act):
                act.wait_ge(filter_ready, 1)
                nc.scalar.copy(filt_sb[:], banks[:, 7, 0:CH]).then_inc(filter_ready, 1)
                act.wait_ge(f_weights, 16 * 8)
                act.wait_ge(f_cleared, 2)
                for b in range(B):
                    def multiply(k, s, t):
                        if not alive(k, k - 1, NC):
                            return
                        rows = height(k, k - 1)
                        g = b * NC + k - 1
                        n = g * T + t
                        if t == 0:
                            act.wait_ge(u_written, (b * C + k) * NBLK if rows == R else (b + 1) * C * NBLK)
                            act.wait_ge(window_ready, g + 1)
                            after(act, out_ready, (g - 1) * OUTS if alive(k, k - 3, NC) else b * NC * OUTS)
                        after(act, added, 2 * (n - T + 1))
                        for i, tap in enumerate(ACT_TAPS):
                            to = y[:, 1 - s, t, :] if i == 0 else z[:, t, i - 1, :]
                            nc.scalar.activation(rows_of(to, rows), shifted(t, 1 - s, tap, rows), ACT.Copy,
                                                 scale=taps[:, t, tap:tap + 1]).then_inc(products, 1)

                    def slot(k, s):
                        for j in range(NBLK):
                            q = (b * C + k) * NBLK + j
                            if block_of(k, j):
                                act.wait_ge(s1_ready, q + 1)
                                after(act, coef_ready, q - 1)
                                nc.scalar.copy(pixels[:, j % 2, :], s1_ps[j % 2]).then_inc(pixels_kept, 1)
                            if block_of(k, j - 2):
                                if j == 2:
                                    past = 0 if isinstance(k, int) and k == 0 else 1
                                    after(act, y_ready, (b * NC + k - past) * T)
                                    after(act, window_ready, b * NC + k)
                                act.wait_ge(inv_ready, q - 1)
                                at = 1 + (j - 2) % NBLK * BLK
                                nc.scalar.copy(u[:, s if j >= 2 else 1 - s, :, 2:UR, at:at + BLK],
                                               inv_ps[j % 2].rearrange("p (t r w) -> p t r w", t=T, r=R)
                                               ).then_inc(u_written, 1)
                            if j in (2, 4, 6):
                                multiply(k, s, j // 2 - 1)
                            if j in (2, 3) and alive(k, k - 2, NC):
                                g = b * NC + k - 2
                                n = height(k, k - 2) * W
                                if j == 2:
                                    act.wait_ge(y_ready, (g + 1) * T)
                                    nc.scalar.activation(y[:, s, 0, 0:n], y[:, s, 0, 0:n], ACT.Gelu)
                                else:
                                    nc.scalar.activation(y[0:REST, s, 2, 0:n], y[0:REST, s, 2, 0:n], ACT.Gelu)
                                    after(act, gated, g)
                                    nc.scalar.copy(aside[:, 0:n], y[REST:2 * REST, s, 2, 0:n]).then_inc(gelu_done, 1)
                    over_slots(act, slot)

            @block.gpsimd
            def _(pool):
                nc.gpsimd.memset(u[:], 0.0).then_inc(f_cleared, 1)
                nc.gpsimd.memset(xr[:], 0.0).then_inc(f_cleared, 1)
                pool.wait_ge(f_cleared, 2)
                for b in range(B):
                    def slot(k, s):
                        if alive(k, k, NC):
                            g = b * NC + k
                            past = g if isinstance(k, int) and k == 0 else g - 1
                            after(pool, y_ready, past * T)
                            after(pool, products, past * T * 3)
                            if isinstance(k, int) and k == 0:
                                nc.gpsimd.memset(u[:, s, :, 0:2, :], 0.0).then_inc(window_ready, 1)
                            else:
                                pool.wait_ge(u_written, (b * C + k) * NBLK)
                                if height(k, k) == 1:
                                    nc.gpsimd.memset(u[:, s, :, 2, :], 0.0)
                                end_waits(pool, passed)
                                nc.gpsimd.tensor_copy(u[:, s, :, 0:2, :], u[:, 1 - s, :, R:UR, :]).then_inc(window_ready, 1)
                        if alive(k, k - 1, NC):
                            size = height(k, k - 1) * W
                            for t in range(T):
                                n = (b * NC + k - 1) * T + t
                                pool.wait_ge(products, 3 * n + 3)
                                for i in range(2):
                                    nc.gpsimd.tensor_tensor(y[:, 1 - s, t, 0:size], y[:, 1 - s, t, 0:size],
                                                            z[:, t, i, 0:size], ALU.add).then_inc(added, 1)
                                    pool.wait_ge(added, 2 * n + i + 1)
                    over_slots(pool, slot)

            @block.vector
            def _(dve):
                dve.wait_ge(f_weights, 16 * 8)
                dve.wait_ge(filter_ready, 2)
                LATE = CHAIN - EARLY - 1
                order = [(0, k) for k in range(EARLY)]
                for t in range(T):
                    for k in range(EARLY, CHAIN):
                        order.append((t, k))
                        if t + 1 < T and k - EARLY < EARLY:
                            order.append((t + 1, k - EARLY))
                ahead = order[:12]
                behind = order[12:]

                def normalise(b, c, s):
                    dve.wait_ge(x_loaded[s], (c - s + b * C) * 8 + 16)
                    after(dve, s1_ready, (b * C + c - 1) * NBLK)
                    for t in range(T):
                        nc.vector.tensor_scalar(
                            xn[:, s, t, :].rearrange("p (j r w) -> p r j w", r=R, w=BLK),
                            xw[:, s, t, :].rearrange("p (r j w) -> p r j w", r=R, w=BLK),
                            gn1[:, b, 0:1], gn1[:, b, 1:2], ALU.subtract, ALU.mult).then_inc(xn_ready, 1)

                normalise(0, 0, 0)
                for b in range(B):
                    def add_taps(k, chunk, s, some):
                        g = b * NC + chunk
                        rows = height(k, chunk)
                        for t, i in some:
                            n = g * T + t
                            if i == 0:
                                dve.wait_ge(added, 2 * n + 2)
                            elif i <= EARLY:
                                dve.wait_ge(early_taps, n * EARLY + i)
                            else:
                                dve.wait_ge(late_taps, n * LATE + i - EARLY)
                            done = early_taps if i < EARLY else late_taps if i < CHAIN - 1 else y_ready
                            tap = DVE_TAPS[i]
                            to = rows_of(y[:, s, t, :], rows)
                            nc.vector.scalar_tensor_tensor(to, shifted(t, s, tap, rows), taps[:, t, tap:tap + 1], to,
                                                           ALU.mult, ALU.add).then_inc(done, 1)

                    def add_residual(k, chunk, s, w):
                        g = b * NC + chunk
                        if w == 0:
                            dve.wait_ge(r_loaded[s], stored(b, s, chunk, s) + 16)
                        dve.wait_ge(out_ready, g * OUTS + w + 1)
                        if height(k, chunk) == 1 and w % 2:
                            dve.wait_ge(summed, g * OUTS + w)
                            dve.sem_inc(summed, 1)
                            return
                        n = HALF if height(k, chunk) == R else W
                        to = xr[:, s, w // 2, w % 2 * HALF:w % 2 * HALF + n]
                        nc.vector.tensor_tensor(to, banks[:, 6 + w % 2, 0:n], to, ALU.add).then_inc(summed, 1)

                    def slot(k, s):
                        for j in range(NBLK):
                            q = (b * C + k) * NBLK + j
                            for w in SUM_LATE.get(j, []) if alive(k, k - 3, NC) else []:
                                add_residual(k, k - 3, 1 - s, w)
                            for w in SUM_AT.get(j, []) if alive(k, k - 2, NC) else []:
                                add_residual(k, k - 2, s, w)
                            if block_of(k, j):
                                dve.wait_ge(coef_ready, q + 1)
                                after(dve, inv_ready, q - 1)
                                nc.vector.tensor_tensor(spectra[:, j % 2, :], coef_ps[j % 2], filt_sb[:],
                                                        ALU.mult).then_inc(filtered, 1)
                            if j < 2 and alive(k, k - 2, NC):
                                add_taps(k, k - 2, s, behind[3 * j:3 * j + 3])
                            if j == 2:
                                if alive(k, k + 1, C):
                                    normalise(b, k + 1, 1 - s)
                                elif isinstance(k, int) and k == C + 1 and b + 1 < B:
                                    normalise(b + 1, 0, 0)
                            if j == 4 and alive(k, k - 2, NC):
                                g = b * NC + k - 2
                                size = height(k, k - 2) * W
                                dve.wait_ge(gelu_done, g + 1)
                                nc.vector.tensor_tensor(y[:, s, 0, 0:size], y[:, s, 0, 0:size], y[:, s, 1, 0:size], ALU.mult)
                                nc.vector.tensor_tensor(y[0:REST, s, 2, 0:size], y[0:REST, s, 2, 0:size],
                                                        aside[:, 0:size], ALU.mult).then_inc(gated, 1)
                            if j >= 3 and alive(k, k - 1, NC):
                                at = [0, 3, 4, 7, 10, 12]
                                add_taps(k, k - 1, 1 - s, ahead[at[j - 3]:at[j - 2]])
                    over_slots(dve, slot)


def kernel(x, L0_conv_w_qkv, L0_conv_w_dw, L0_conv_w_proj, L0_conv_temperature, L0_conv_a1, L0_conv_a2,
           L0_conv_a3, L0_conv_a4, L1_conv_fft_filter, L1_conv_w_in, L1_conv_w_dw, L1_conv_w_out):
    import concourse.bacc as _bacc
    from concourse.bass_utils import run_bass_kernel_spmd as _run

    half = CH // 2
    hidden = [*range(0, P), *range(half, half + P), *range(P, half), *range(half + P, CH)]
    columns = [T * m + t for t in range(T) for m in range(P)]
    forward, inverse, spread = spectrum_constants()
    group = (np.arange(P)[:, None] // (GROUP // T) == np.arange(P)[None, :] // (GROUP // T))
    arrays = {
        "x": x,
        "wqkv": L0_conv_w_qkv.T,
        "wdw0": L0_conv_w_dw.reshape(3 * CH, 9),
        "wproj": L0_conv_w_proj.T[:, columns],
        "temperature": L0_conv_temperature,
        "a1": L0_conv_a1, "a2": L0_conv_a2, "a3": L0_conv_a3, "a4": L0_conv_a4,
        "filt": L1_conv_fft_filter.reshape(CH, -1).T[:, hidden],
        "win": L1_conv_w_in.T[:, hidden],
        "wdw1": L1_conv_w_dw.reshape(CH, 9)[hidden],
        "wout": L1_conv_w_out.T[:, columns],
        "identity": np.eye(P, dtype=np.float32),
        "group": group.astype(np.float32) * np.float32(T / GROUP),
        "forward": forward, "inverse": inverse, "spread": spread,
    }
    arrays = {f"in_{name}": np.ascontiguousarray(a) for name, a in arrays.items()}
    nc = _bacc.Bacc("TRN2", target_bir_lowering=False, num_devices=1)
    args = [nc.dram_tensor(name, a.shape, mybir.dt.from_np(a.dtype), kind="ExternalInput").ap()
            for name, a in arrays.items()]
    out = nc.dram_tensor("out", x.shape, F32, kind="ExternalOutput").ap()
    two_layers(nc, *args, out)
    r = _run(nc, [arrays], core_ids=[0])
    return r.results[0]["out"]
```

```python
from contextlib import ExitStack

import numpy as np

import concourse.bass as bass
from concourse import mybir

F32 = mybir.dt.float32
F32R = mybir.dt.float32r
ALU = mybir.AluOpType
ACT = mybir.ActivationFunctionType
AX_X = mybir.AxisListType.X

P = 128
B = 2
CH = 384
T = CH // P
W = 128
HEADS = 8
HC = CH // HEADS
PAIRS = HEADS // 2
SLOT = 64
R = 8
CW = R * W
HALF = CW // 2
UR, UW = R + 2, W + 2
QT = 3 * CH // P
KT = 2 * CH // P
GROUP = 12
BLK = P // R
NBLK = W // BLK
GN_EPS = 1e-5
TOPK = [HC // 2, HC * 2 // 3, HC * 3 // 4, HC * 4 // 5]
LEAD = QT - 1
RT = QT - 1
RING = 4
LOWEST = -3.0e38
ACT_TAPS = [4, 0, 2]
DVE_TAPS = [1, 3, 5, 6, 7, 8]


def after(engine, semaphore, value):
    if not isinstance(value, int) or value > 0:
        engine.wait_ge(semaphore, value)


def end_waits(engine, passed):
    engine.sem_inc(passed, 1)


def over_chunks(engine, chunks, body, alone=1):
    for c in range(2 * alone):
        body(c, c % 2)
    with engine.Fori(alone, chunks // 2 - 1) as pair:
        for s in (0, 1):
            body(2 * pair + s, s)
    for c in (chunks - 2, chunks - 1):
        body(c, c % 2)


def spectrum_constants():
    fwd, inv, sel = [], [], []
    y, x = np.meshgrid(np.arange(R), np.arange(R), indexing="ij")
    for ky in range(R // 2 + 1):
        edge = ky in (0, R // 2)
        for kx in range(R // 2 + 1 if edge else R):
            angle = 2 * np.pi * ((kx * y + ky * x) % R) / R
            alone = edge and kx in (0, R // 2)
            pick = np.zeros((R, R // 2 + 1))
            pick[kx, ky] += 0.5
            pick[(-kx) % R if edge else kx, ky] += 0.5
            for part in (np.cos(angle),) if alone else (np.cos(angle), -np.sin(angle)):
                fwd.append(part)
                inv.append(part * (1 if alone else 2) / R**2)
                sel.append(pick.ravel())
    fwd, inv, sel = np.array(fwd), np.array(inv), np.array(sel)
    n = len(fwd)
    forward = np.zeros((R, 2, R, 2, n))
    inverse = np.zeros((2, n, R, 2, R))
    for p in range(2):
        forward[:, p, :, p, :] = fwd.transpose(1, 2, 0)
        inverse[p, :, :, p, :] = inv
    spread = np.concatenate([sel, sel], 0).T
    return (forward.reshape(P, P).astype(np.float32), inverse.reshape(P, P).astype(np.float32),
            np.ascontiguousarray(spread, np.float32))


def norm_coefficients(nc, ctx, name, partials, group_avg, psum, out):
    def sem(what):
        return ctx.enter_context(nc.semaphore(f"{name}_{what}"))

    step, avg_in, avg_out, dev_in, dev_out, root = (
        sem(w) for w in ("step", "avg_in", "avg_out", "dev_in", "dev_out", "root"))
    own = ctx.enter_context(nc.sbuf_tensor(f"{name}_own", [P, B, 2], F32))
    dev = ctx.enter_context(nc.sbuf_tensor(f"{name}_dev", [P, B], F32))
    var = ctx.enter_context(nc.sbuf_tensor(f"{name}_var", [P, B], F32))
    std = ctx.enter_context(nc.sbuf_tensor(f"{name}_std", [P, B], F32))
    tmp = ctx.enter_context(nc.sbuf_tensor(f"{name}_tmp", [P, B], F32))

    def vector(dve):
        count = [0]

        def then_wait(instruction):
            count[0] += 1
            instruction.then_inc(step, 1)
            dve.wait_ge(step, count[0])

        for b in range(B):
            then_wait(nc.vector.bn_aggr(own[:, b, :], partials[:, b, :]))
        dve.sem_inc(avg_in, 1)
        dve.wait_ge(avg_out, 1)
        then_wait(nc.vector.tensor_copy(out[:, :, 0], psum[:, 0:2 * B].rearrange("p (b s) -> p b s", b=B)[:, :, 0]))
        then_wait(nc.vector.tensor_copy(var[:], psum[:, 0:2 * B].rearrange("p (b s) -> p b s", b=B)[:, :, 1]))
        then_wait(nc.vector.tensor_tensor(tmp[:], own[:, :, 0], out[:, :, 0], ALU.subtract))
        then_wait(nc.vector.tensor_tensor(dev[:], tmp[:], tmp[:], ALU.mult))
        dve.sem_inc(dev_in, 1)
        dve.wait_ge(dev_out, 1)
        then_wait(nc.vector.tensor_tensor(tmp[:], var[:], psum[:, 8:8 + B], ALU.add))
        nc.vector.tensor_scalar(var[:], tmp[:], GN_EPS, None, ALU.add).then_inc(root, 1)
        dve.wait_ge(root, 2)
        then_wait(nc.vector.reciprocal(std[:], dev[:]))
        then_wait(nc.vector.tensor_tensor(tmp[:], std[:], std[:], ALU.mult))
        then_wait(nc.vector.tensor_tensor(dev[:], tmp[:], var[:], ALU.mult))
        then_wait(nc.vector.tensor_scalar(tmp[:], dev[:], -0.5, 1.5, ALU.mult, ALU.add))
        then_wait(nc.vector.tensor_tensor(out[:, :, 1], tmp[:], std[:], ALU.mult))

    def tensor(pe):
        pe.wait_ge(avg_in, 1)
        nc.tensor.matmul(psum[:, 0:2 * B], group_avg[:], own[:].rearrange("p b s -> p (b s)"),
                         start=True, stop=True).then_inc(avg_out, 1)
        pe.wait_ge(dev_in, 1)
        nc.tensor.matmul(psum[:, 8:8 + B], group_avg[:], dev[:], start=True, stop=True).then_inc(dev_out, 1)

    def scalar(act):
        act.wait_ge(root, 1)
        nc.scalar.activation(dev[:], var[:], ACT.Sqrt).then_inc(root, 1)

    return vector, tensor, scalar


def two_layers(nc, x, wqkv, wdw0, wproj, temperature, a1, a2, a3, a4, filt, win, wdw1, wout,
               identity_in, group_in, forward_in, inverse_in, spread_in, out):
    H = x.shape[2]
    C = H // R
    xv, ov = (a.rearrange("b (p t) h w -> b p t (h w)", t=T) for a in (x, out))
    v_d = nc.dram_tensor("v_scratch", [B, T, P, (H + R) * W], F32).ap()
    x1_d = nc.dram_tensor("x1_scratch", [B, P, T, H * W], F32).ap()
    gram_d = nc.dram_tensor("gram_scratch", [B, PAIRS, 2 * HC, 2 * HC], F32).ap()
    norm_d = nc.dram_tensor("norm_scratch", [B, KT * P], F32).ap()
    mix_d = nc.dram_tensor("mix_scratch", [B, CH, CH], F32).ap()

    with ExitStack() as whole:
        def keep(name, shape):
            return whole.enter_context(nc.sbuf_tensor(name, shape, F32))

        banks = whole.enter_context(nc.psum_tensor("banks", [P, 8, 512], F32))
        gn0, gn1 = keep("gn0", [P, B, 2]), keep("gn1", [P, B, 2])
        group_avg = keep("group_avg", [P, P])
        identity = keep("identity", [P, P])
        gram = keep("gram", [P, B, PAIRS * 2 * HC])
        squares = keep("squares", [P, B, KT, C + 1])

        with ExitStack() as ctx:
            def sb(name, shape):
                return ctx.enter_context(nc.sbuf_tensor(name, shape, F32))

            def sem(name):
                return ctx.enter_context(nc.semaphore(name))

            PIECES = C // 2
            xs = sb("st_x", [P, 2, T, 2 * CW])
            partials = sb("st_partials", [P, B, C * T * 12])
            st_loaded = [sem("st_loaded0"), sem("st_loaded1")]
            consts_loaded, st_used, passed = sem("st_consts"), sem("st_used"), sem("st_passed")
            block = ctx.enter_context(nc.Block())
            vector, tensor, scalar = norm_coefficients(nc, ctx, "gn0", partials, group_avg,
                                                       banks[:, 0, :], gn0)

            @block.sync
            def _(sp):
                sp.dma_start(group_avg[:], group_in).then_inc(consts_loaded, 16)
                sp.dma_start(identity[:], identity_in).then_inc(consts_loaded, 16)
                for b in range(B):
                    def load(c, s):
                        after(sp, st_used, b * PIECES + c - 1)
                        end_waits(sp, passed)
                        sp.dma_start(xs[:, s], xv[b][:, :, bass.ds(c * (2 * CW), 2 * CW)]).then_inc(st_loaded[s], 16)
                    over_chunks(sp, PIECES, load)
                sp.wait_ge(consts_loaded, 32)

            @block.vector
            def _(dve):
                for b in range(B):
                    def stats(c, s):
                        dve.wait_ge(st_loaded[s], (c - s + b * PIECES) * 8 + 16)
                        for t in range(T):
                            for h in range(4):
                                last = nc.vector.bn_stats(
                                    partials[:, b, bass.ds(c * (T * 24) + (t * 4 + h) * 6, 6)],
                                    xs[:, s, t, h * HALF:(h + 1) * HALF])
                        last.then_inc(st_used, 1)
                    over_chunks(dve, PIECES, stats)
                dve.wait_ge(st_used, B * PIECES)
                vector(dve)

            @block.tensor
            def _(pe):
                pe.wait_ge(consts_loaded, 32)
                tensor(pe)

            @block.scalar
            def _(act):
                scalar(act)

        with ExitStack() as ctx:
            def sb(name, shape, dtype=F32):
                return ctx.enter_context(nc.sbuf_tensor(name, shape, dtype))

            def sem(name):
                return ctx.enter_context(nc.semaphore(name))

            w_high, w_low = sb("wq_high", [P, T, 3 * CH], F32R), sb("wq_low", [P, T, 3 * CH], F32R)
            taps = sb("taps0", [P, QT, 9])
            xs = sb("a_x", [P, T, CW])
            x_high, x_low = sb("x_high", [P, 2, T, CW], F32R), sb("x_low", [P, 2, T, CW], F32R)
            u = sb("u", [P, RING, UR, UW])
            lead_u = sb("lead_u", [P, UR, UW])
            lead_diag = sb("lead_diag", [P, 9, P])
            carry = sb("carry", [P, QT, 2, W])
            z = sb("z", [P, 2, 3, CW])
            y = sb("y", [P, RING, CW])
            lead_y = sb("lead_y", [P, CW])
            junk = sb("junk", [P, CW])
            qkT = sb("qkT", [P, 2, R, CH])
            up = [banks[:, 2 * i:2 * i + 2, :].rearrange("p a n -> p (a n)") for i in range(2)]
            turned = banks[:, 4:6, :].rearrange("p a n -> p (a n)")
            gram_ps = banks[0:2 * HC, 6, 0:PAIRS * 2 * HC]
            lead_ps = banks[:, 7, :]

            weights_loaded, split = sem("a_weights"), sem("a_split")
            x_loaded = sem("a_x_loaded")
            passed = sem("a_passed")
            cleared = sem("a_cleared")
            normalised = sem("a_normalised")
            high_ready = sem("a_high")
            xn_ready = sem("a_xn")
            up_ready = sem("a_up")
            u_written = sem("a_u")
            carried_out = sem("a_carried_out")
            carried_in = sem("a_carried_in")
            products = sem("a_products")
            added = sem("a_added")
            lead_written = sem("a_lead_u")
            lead_carried_in = sem("a_lead_in")
            lead_ready = sem("a_lead")
            lead_kept = sem("a_lead_kept")
            early_taps = sem("a_early_taps")
            late_taps = sem("a_late_taps")
            cut = sem("a_cut")
            y_ready = sem("a_y")
            squared = sem("a_squared")
            turned_ready = sem("a_turned")
            turned_kept = sem("a_turned_kept")
            gram_ready = sem("a_gram")
            gram_added = sem("a_gram_added")
            v_stored = [sem(f"a_v{i}") for i in range(T)]
            block = ctx.enter_context(nc.Block())

            NC = C + 1
            CHAIN = len(DVE_TAPS)
            EARLY = CHAIN // 2
            NORM_AT = 5
            SPLIT_AT = [2, 3, 4]
            GRAM_AT = 3
            LEAD_AT = [1, 2, 4, 5, 6, 7]

            def shifted(t, tap, rows):
                dy, dx = tap // 3, tap % 3
                return u[:, t % RING, dy:dy + rows, dx:dx + W]

            def image(ap, rows):
                return ap[:, 0:rows * W].rearrange("p (r w) -> p r w", w=W)

            def wait_slot_read(engine, g, t):
                g, tile = (g, t - RING) if t >= RING else (g - 1, t - RING + RT)
                if tile < KT:
                    after(engine, turned_ready, g * KT + tile + 1)
                    after(engine, squared, g * KT + tile + 1)
                else:
                    after(engine, v_stored[tile - KT], (g + 1) * 16)

            @block.sync
            def _(sp):
                raw = z[:].rearrange("p a b n -> p (a b n)")[:, 0:T * 3 * CH].rearrange("p (t o) -> p t o", t=T)
                sp.dma_start(raw, wqkv.rearrange("(p t) o -> p t o", t=T)).then_inc(weights_loaded, 16)
                sp.dma_start(taps[:], wdw0.rearrange("(t p) k -> p t k", p=P)).then_inc(weights_loaded, 16)

                def load(b, c):
                    after(sp, xn_ready, (b * C + c) * T)
                    end_waits(sp, passed)
                    sp.dma_start(xs[:], xv[b][:, :, bass.ds(c * CW, CW)]).then_inc(x_loaded, 16)

                def store_v(b, c, rows):
                    g = b * NC + c
                    sp.wait_ge(lead_kept, 2 * g + 2)
                    end_waits(sp, passed)
                    sp.dma_start(v_d[b, LEAD - KT][:, bass.ds(c * CW, rows * W)],
                                 lead_y[:, 0:rows * W]).then_inc(v_stored[LEAD - KT], 16)
                    for t in range(KT, RT):
                        sp.wait_ge(y_ready, g * RT + t + 1)
                        end_waits(sp, passed)
                        sp.dma_start(v_d[b, t - KT][:, bass.ds(c * CW, rows * W)],
                                     y[:, t % RING, 0:rows * W]).then_inc(v_stored[t - KT], 16)

                load(0, 0)
                load(0, 1)
                for b in range(B):
                    def chunk(c, s):
                        if not (isinstance(c, int) and c >= C - 2):
                            load(b, c + 2)
                        elif c == C - 2 and b + 1 < B:
                            load(b + 1, 0)
                        store_v(b, c, R)
                    over_chunks(sp, C, chunk)
                    if b + 1 < B:
                        load(b + 1, 1)
                    store_v(b, C, 1)
                for t in range(T):
                    sp.wait_ge(v_stored[t], B * NC * 16)

            @block.tensor
            def _(pe):
                pe.wait_ge(split, 3)
                for b in range(B):
                    def turn(c, t, rows):
                        g = b * NC + c
                        pe.wait_ge(y_ready, g * RT + t + 1)
                        after(pe, turned_kept, g * KT + t)
                        for i in range(rows):
                            last = nc.tensor.transpose(turned[:, i * P:(i + 1) * P],
                                                       y[:, t % RING, i * W:(i + 1) * W], identity[:])
                        last.then_inc(turned_ready, 1)

                    def multiply_gram(c, rows):
                        g = b * NC + c
                        pe.wait_ge(turned_kept, (g + 1) * KT)
                        after(pe, gram_added, g)
                        for p in range(PAIRS):
                            pair = slice(p * 2 * HC, (p + 1) * 2 * HC)
                            for i in range(rows):
                                last = nc.tensor.matmul(gram_ps[:, pair], qkT[:, 0, i, pair], qkT[:, 1, i, pair],
                                                        start=(i == 0), stop=(i == rows - 1))
                        last.then_inc(gram_ready, 1)

                    def lead_taps(c, half, dys, rows):
                        g = b * NC + c
                        if dys[0] == 0:
                            pe.wait_ge(lead_written, g + 1)
                            pe.wait_ge(lead_carried_in, g + 1)
                            after(pe, lead_kept, 2 * g + half)
                        to = lead_ps[:, 0:rows * W].rearrange("p (r w) -> p r w", w=W)
                        for dy in dys:
                            for dx in range(3):
                                top = half * (R // 2) + dy
                                last = nc.tensor.matmul(to, lead_diag[:, dy * 3 + dx, :],
                                                        lead_u[:, top:top + rows, dx:dx + W],
                                                        start=(dy == dx == 0), stop=(dy == dx == 2))
                        if dys[-1] == 2:
                            last.then_inc(lead_ready, 2 if rows == 1 else 1)

                    def project(c, s, tile, step):
                        m = (b * C + c) * QT + step
                        after(pe, carried_out, m - 1)
                        for h in range(2):
                            to = up[(s * QT + step) % 2][:, h * HALF:(h + 1) * HALF]
                            for k in range(T):
                                for i, (w, xp) in enumerate(((w_high, x_high), (w_low, x_high), (w_high, x_low))):
                                    last = nc.tensor.matmul(
                                        to, w[:, k, tile * P:(tile + 1) * P], xp[:, s, k, h * HALF:(h + 1) * HALF],
                                        start=(k == 0 and i == 0), stop=(k == T - 1 and i == 2))
                        last.then_inc(up_ready, 1)

                    def chunk(c, s):
                        first = isinstance(c, int) and c == 0
                        pe.wait_ge(xn_ready, (b * C + c + 1) * T)
                        project(c, s, LEAD, 0)
                        for t in range(RT):
                            project(c, s, t, t + 1)
                            if t > RING:
                                turn(c, t - RING - 1, R)
                            elif RT - RING + t - 1 < KT and not first:
                                turn(c - 1, RT - RING + t - 1, R)
                            elif t == GRAM_AT and not first:
                                multiply_gram(c - 1, R)
                            for piece in [i for i, at in enumerate(LEAD_AT) if at == t]:
                                lead_taps(c, piece // 3, [piece % 3], R // 2)
                    over_chunks(pe, C, chunk)
                    for t in range(RT - RING - 1, KT):
                        turn(C - 1, t, R)
                    multiply_gram(C - 1, R)
                    lead_taps(C, 0, [0, 1, 2], 1)
                    for t in range(KT):
                        turn(C, t, 1)
                    multiply_gram(C, 1)

            @block.scalar
            def _(act):
                act.wait_ge(weights_loaded, 32)
                act.wait_ge(cleared, 3)

                def split_high(i, s, k):
                    act.wait_ge(normalised, i + 1)
                    after(act, up_ready, (i - 1) * QT)
                    nc.scalar.copy(x_high[:, s, k], xs[:, k]).then_inc(high_ready, 1)

                for k in range(T):
                    split_high(0, 0, k)
                for b in range(B):
                    def keep(c, t, rows):
                        g = b * NC + c
                        act.wait_ge(turned_ready, g * KT + t + 1)
                        after(act, gram_ready, g)
                        nc.scalar.copy(qkT[:, t // T, 0:rows, t % T * P:(t % T + 1) * P],
                                       turned[:, 0:rows * P].rearrange("p (r d) -> p r d", d=P)).then_inc(turned_kept, 1)

                    def square(c, t, rows):
                        q = (b * NC + c) * KT + t
                        act.wait_ge(y_ready, (b * NC + c) * RT + t + 1)
                        after(act, squared, q)
                        nc.scalar.activation(junk[:, 0:rows * W], y[:, t % RING, 0:rows * W], ACT.Square,
                                             accum_out=squares[:, b, t, bass.ds(c, 1)]).then_inc(squared, 1)

                    def multiply(c, t, rows):
                        g = b * NC + c
                        n = g * RT + t
                        act.wait_ge(u_written, n + 1)
                        act.wait_ge(carried_in, n + 1)
                        after(act, added, 2 * (n - 1))
                        for k, tap in enumerate(ACT_TAPS):
                            nc.scalar.activation(image(z[:, t % 2, k, :], rows), shifted(t, tap, rows), ACT.Copy,
                                                 scale=taps[:, t, tap:tap + 1]).then_inc(products, 1)

                    def take_lead(c, s):
                        g = b * NC + c
                        m = (b * C + c) * QT
                        act.wait_ge(up_ready, m + 1)
                        after(act, lead_ready, 2 * g)
                        rows_in = up[s * QT % 2].rearrange("p (r w) -> p r w", w=W)
                        nc.scalar.copy(lead_u[:, 2:UR, 1:1 + W], rows_in).then_inc(lead_written, 1)
                        act.wait_ge(lead_carried_in, g + 1)
                        nc.scalar.copy(carry[:, LEAD, :, :], rows_in[:, R - 2:R, :]).then_inc(carried_out, 1)

                    def keep_lead(c, half, pixels):
                        g = b * NC + c
                        act.wait_ge(lead_ready, 2 * g + half + 1)
                        after(act, v_stored[LEAD - KT], g * 16)
                        nc.scalar.copy(lead_y[:, half * HALF:half * HALF + pixels],
                                       lead_ps[:, 0:pixels]).then_inc(lead_kept, 1)

                    def chunk(c, s):
                        first = isinstance(c, int) and c == 0
                        take_lead(c, s)
                        for t in range(RT):
                            g = b * NC + c
                            n = g * RT + t
                            m = (b * C + c) * QT + t + 1
                            act.wait_ge(up_ready, m + 1)
                            after(act, y_ready, n - RING + 1)
                            rows_in = up[(s * QT + t + 1) % 2].rearrange("p (r w) -> p r w", w=W)
                            nc.scalar.copy(u[:, t % RING, 2:UR, 1:1 + W], rows_in).then_inc(u_written, 1)
                            act.wait_ge(carried_in, n + 1)
                            nc.scalar.copy(carry[:, t, :, :], rows_in[:, R - 2:R, :]).then_inc(carried_out, 1)
                            multiply(c, t, R)
                            if t in SPLIT_AT and not (isinstance(c, int) and c == C - 1):
                                split_high(b * C + c + 1, 1 - s, SPLIT_AT.index(t))
                            if t >= RING:
                                square(c, t - RING, R)
                            elif RT + t - RING < KT and not first:
                                square(c - 1, RT + t - RING, R)
                            if t > RING:
                                keep(c, t - RING - 1, R)
                            elif RT - RING + t - 1 < KT and not first:
                                keep(c - 1, RT - RING + t - 1, R)
                            if t in (LEAD_AT[2], LEAD_AT[5]):
                                keep_lead(c, 0 if t == LEAD_AT[2] else 1, HALF)
                    over_chunks(act, C, chunk)
                    for t in range(RT):
                        if t < KT + RING - RT:
                            square(C - 1, RT + t - RING, R)
                        if t == 0:
                            for i in range(RT - RING - 1, KT):
                                keep(C - 1, i, R)
                        multiply(C, t, 1)
                        if t == 0:
                            keep_lead(C, 0, W)
                            act.sem_inc(lead_kept, 1)
                        if 2 <= t < KT + 2:
                            square(C, t - 2, 1)
                            keep(C, t - 2, 1)
                        if t in SPLIT_AT and b + 1 < B:
                            split_high((b + 1) * C, 0, SPLIT_AT.index(t))

            @block.gpsimd
            def _(pool):
                nc.gpsimd.memset(u[:], 0.0).then_inc(cleared, 1)
                nc.gpsimd.memset(lead_u[:], 0.0).then_inc(cleared, 1)
                nc.gpsimd.memset(gram[:], 0.0).then_inc(cleared, 1)
                pool.wait_ge(cleared, 3)

                def carry_in(b, c, t):
                    n = (b * NC + c) * RT + t
                    after(pool, y_ready, n - RING + 1)
                    top = u[:, t % RING, 0:2, 1:1 + W]
                    if isinstance(c, int) and c == 0:
                        nc.gpsimd.memset(top, 0.0).then_inc(carried_in, 1)
                        return
                    pool.wait_ge(carried_out, (b * C + c - 1) * QT + t + 2)
                    if isinstance(c, int) and c == C:
                        pool.wait_ge(u_written, n)
                        nc.gpsimd.memset(u[:, t % RING, 2, 1:1 + W], 0.0).then_inc(u_written, 1)
                    end_waits(pool, passed)
                    nc.gpsimd.tensor_copy(top, carry[:, t, :, :]).then_inc(carried_in, 1)

                def carry_lead_in(b, c):
                    g = b * NC + c
                    after(pool, lead_ready, 2 * g)
                    top = lead_u[:, 0:2, 1:1 + W]
                    if isinstance(c, int) and c == 0:
                        nc.gpsimd.memset(top, 0.0).then_inc(lead_carried_in, 1)
                        return
                    pool.wait_ge(carried_out, (b * C + c - 1) * QT + 1)
                    if isinstance(c, int) and c == C:
                        pool.wait_ge(lead_written, g)
                        nc.gpsimd.memset(lead_u[:, 2, 1:1 + W], 0.0).then_inc(lead_written, 1)
                    end_waits(pool, passed)
                    nc.gpsimd.tensor_copy(top, carry[:, LEAD, :, :]).then_inc(lead_carried_in, 1)

                def split_low(i, s, k):
                    pool.wait_ge(high_ready, i * T + k + 1)
                    after(pool, up_ready, (i - 1) * QT)
                    nc.gpsimd.tensor_tensor(x_low[:, s, k], xs[:, k], x_high[:, s, k].bitcast(F32),
                                            ALU.subtract).then_inc(xn_ready, 1)

                for k in range(T):
                    split_low(0, 0, k)
                carry_lead_in(0, 0)
                carry_in(0, 0, 0)
                for b in range(B):
                    def steps(c, s, rows):
                        fixed = isinstance(c, int)
                        for t in range(RT):
                            n = (b * NC + c) * RT + t
                            if t + 1 < RT:
                                carry_in(b, c, t + 1)
                            elif not (fixed and c == C):
                                carry_lead_in(b, c + 1)
                                carry_in(b, c + 1, 0)
                            elif b + 1 < B:
                                carry_lead_in(b + 1, 0)
                                carry_in(b + 1, 0, 0)
                            pool.wait_ge(products, 3 * n + 3)
                            wait_slot_read(pool, b * NC + c, t)
                            to = y[:, t % RING, 0:rows * W]
                            first, second, third = (z[:, t % 2, k, 0:rows * W] for k in range(3))
                            nc.gpsimd.tensor_tensor(to, first, second, ALU.add).then_inc(added, 1)
                            pool.wait_ge(added, 2 * n + 1)
                            nc.gpsimd.tensor_tensor(to, to, third, ALU.add).then_inc(added, 1)
                            if t in SPLIT_AT:
                                if not (fixed and c >= C - 1):
                                    split_low(b * C + c + 1, 1 - s, SPLIT_AT.index(t))
                                elif c == C and b + 1 < B:
                                    split_low((b + 1) * C, 0, SPLIT_AT.index(t))

                    over_chunks(pool, C, lambda c, s: steps(c, s, R))
                    steps(C, 0, 1)

            @block.vector
            def _(dve):
                dve.wait_ge(weights_loaded, 32)
                raw = z[:].rearrange("p a b n -> p (a b n)")[:, 0:T * 3 * CH].rearrange("p (t o) -> p t o", t=T)
                nc.vector.tensor_copy(w_high[:], raw).then_inc(split, 1)
                dve.wait_ge(split, 1)
                nc.vector.tensor_tensor(w_low[:], raw, w_high[:].bitcast(F32), ALU.subtract).then_inc(split, 1)
                for k in range(9):
                    last = nc.vector.tensor_scalar(lead_diag[:, k, :], identity[:], taps[:, LEAD, k:k + 1], None, ALU.mult)
                last.then_inc(split, 1)
                dve.wait_ge(cleared, 3)

                def normalise(b, c):
                    dve.wait_ge(x_loaded, 16 * (b * C + c + 1))
                    nc.vector.tensor_scalar(xs[:], xs[:], gn0[:, b, 0:1], gn0[:, b, 1:2],
                                            ALU.subtract, ALU.mult).then_inc(normalised, 1)

                def add_gram(b, c):
                    dve.wait_ge(gram_ready, b * NC + c + 1)
                    after(dve, gram_added, b * NC + c)
                    total = gram[0:2 * HC, b, :]
                    nc.vector.tensor_tensor(total, total, gram_ps, ALU.add).then_inc(gram_added, 1)

                def add_tap(b, c, t, k, rows):
                    n = (b * NC + c) * RT + t
                    if k == 0:
                        dve.wait_ge(added, 2 * n + 2)
                    elif k <= EARLY:
                        dve.wait_ge(early_taps, n * EARLY + k)
                    else:
                        dve.wait_ge(late_taps, n * (CHAIN - EARLY - 1) + k - EARLY)
                    done = (early_taps if k < EARLY else late_taps if k < CHAIN - 1
                            else cut if isinstance(c, int) and c == 0 else y_ready)
                    to = image(y[:, t % RING, :], rows)
                    tap = DVE_TAPS[k]
                    nc.vector.scalar_tensor_tensor(to, shifted(t, tap, rows), taps[:, t, tap:tap + 1], to,
                                                   ALU.mult, ALU.add).then_inc(done, 1)

                normalise(0, 0)
                for k in range(EARLY):
                    add_tap(0, 0, 0, k, R)
                normalise(0, 1)
                for b in range(B):
                    def steps(c, s, rows):
                        fixed = isinstance(c, int)
                        for t in range(RT):
                            if t + 1 < RT:
                                following = (b, c, t + 1, rows)
                            elif not (fixed and c == C):
                                following = (b, c + 1, 0, 1 if fixed and c + 1 == C else R)
                            else:
                                following = (b + 1, 0, 0, R) if b + 1 < B else None
                            for k in range(EARLY, CHAIN):
                                add_tap(b, c, t, k, rows)
                                if following:
                                    fb, fc, ft, frows = following
                                    add_tap(fb, fc, ft, k - EARLY, frows)
                            to = image(y[:, t % RING, :], rows)
                            if fixed and c == 0:
                                dve.wait_ge(cut, b * RT + t + 1)
                                nc.vector.memset(to[:, 0, :], 0.0).then_inc(y_ready, 1)
                            if t == 5 and not (fixed and c == 0):
                                add_gram(b, c - 1)
                            if t == NORM_AT:
                                if not (fixed and c >= C - 2):
                                    normalise(b, c + 2)
                                elif c == C - 2 and b + 1 < B:
                                    normalise(b + 1, 0)
                                elif c == C and b + 1 < B:
                                    normalise(b + 1, 1)

                    over_chunks(dve, C, lambda c, s: steps(c, s, R))
                    steps(C, 0, 1)
                    add_gram(b, C)

        with ExitStack() as ctx:
            def sb(name, shape):
                return ctx.enter_context(nc.sbuf_tensor(name, shape, F32))

            def sem(name):
                return ctx.enter_context(nc.semaphore(name))

            NB = B * PAIRS
            K4 = len(TOPK)
            ssq, rn, nt0, nt1 = (sb(n, [P, B * KT]) for n in ("ssq", "rn", "nt0", "nt1"))
            qn = sb("qn", [P, B, PAIRS])
            kn = sb("kn", [P, B, PAIRS, HC])
            temp = sb("temp", [P, PAIRS])
            gains = sb("gains", [P, K4])
            qk = sb("qk", [P, NB, HC])
            scaled = sb("scaled", [P, NB, HC])
            logits = sb("logits", [P, NB, HC])
            left = sb("left", [P, NB, HC])
            tops = sb("tops", [P, NB, 40])
            lowered = sb("lowered", [P, NB])
            expd = sb("expd", [P, NB, HC])
            masked = sb("masked", [P, K4, NB, HC])
            sums = sb("sums", [P, K4, NB])
            shares = sb("shares", [P, K4, NB])
            mixed = sb("mixed", [P, NB, HC])
            diag = sb("diag", [P, NB, P])
            wp = sb("wp", [P, PAIRS, CH])
            mt = sb("mt", [P, NB, CH])
            t_moved = sem("t_moved")
            t_loaded, t_norm, t_back = sem("t_loaded"), sem("t_norm"), sem("t_back")
            t_zeroed, t_chain, t_root = sem("t_zeroed"), sem("t_chain"), sem("t_root")
            t_exp, t_diag, t_mt, t_mt_kept, t_stored = (
                sem(n) for n in ("t_exp", "t_diag", "t_mt", "t_mt_kept", "t_stored"))
            block = ctx.enter_context(nc.Block())

            @block.sync
            def _(sp):
                with nc.allow_non_contiguous_dma(reason="tables of a few hundred numbers"):
                    wpv = wproj.rearrange("(p s i) o -> s i p o", s=2, i=HC)
                    tv = temperature.rearrange("(p s) a b -> s (a b) p", s=2)
                    sp.wait_ge(t_zeroed, 1)
                    for s in range(2):
                        sp.dma_start(wp[s * SLOT:s * SLOT + HC], wpv[s]).then_inc(t_loaded, 16)
                        sp.dma_start(temp[s * SLOT:(s + 1) * SLOT], tv[s].to_broadcast([SLOT, PAIRS])).then_inc(t_loaded, 16)
                    for i, a in enumerate((a1, a2, a3, a4)):
                        sp.dma_start(gains[:, i:i + 1], a.rearrange("(a b) -> a b", a=1).to_broadcast([P, 1])).then_inc(t_loaded, 16)
                    for b in range(B):
                        sp.dma_start(gram_d[b].rearrange("r i j -> i r j"),
                                     gram[0:2 * HC, b, :].rearrange("p (r j) -> p r j", r=PAIRS)).then_inc(t_moved, 16)
                    sp.wait_ge(t_norm, 1)
                    for b in range(B):
                        sp.dma_start(norm_d[b].rearrange("(t p) -> p t", p=P), rn[:, b * KT:(b + 1) * KT]).then_inc(t_back, 16)
                    sp.wait_ge(t_back, 16 * B)
                    sp.wait_ge(t_moved, 16 * B)
                    for n in range(NB):
                        for s in range(2):
                            own = slice(s * HC, (s + 1) * HC)
                            sp.dma_start(qk[s * SLOT:s * SLOT + HC, n, :], gram_d[n // PAIRS, n % PAIRS][own, own]
                                         ).then_inc(t_moved, 16)
                    for b in range(B):
                        nq = norm_d[b, 0:CH].rearrange("(p s i) -> s i p", s=2, i=HC)
                        nk = norm_d[b, CH:2 * CH].rearrange("(a p s i) -> s a p i", a=1, s=2, i=HC)
                        for s in range(2):
                            sp.dma_start(qn[s * SLOT:s * SLOT + HC, b, :], nq[s]).then_inc(t_back, 16)
                            sp.dma_start(kn[s * SLOT:(s + 1) * SLOT, b], nk[s].to_broadcast([SLOT, PAIRS, HC])).then_inc(t_back, 16)
                for n in range(NB):
                    b, p = n // PAIRS, n % PAIRS
                    sp.wait_ge(t_mt_kept, n + 1)
                    for s in range(2):
                        row = (2 * p + s) * HC
                        sp.dma_start(mix_d[b, row:row + HC, :], mt[s * SLOT:s * SLOT + HC, n, :]).then_inc(t_stored, 16)
                sp.wait_ge(t_stored, 16 * 2 * NB)

            @block.scalar
            def _(act):
                act.wait_ge(t_root, 1)
                nc.scalar.activation(nt0[:], ssq[:], ACT.Sqrt).then_inc(t_root, 1)
                act.wait_ge(t_exp, 1)
                for n in range(NB):
                    last = nc.scalar.activation(expd[:, n, :], logits[:, n, :], ACT.Exp, bias=lowered[:, n:n + 1])
                last.then_inc(t_exp, 1)
                for n in range(NB):
                    act.wait_ge(t_mt, n + 1)
                    nc.scalar.copy(mt[:, n, :], banks[:, n, 0:CH]).then_inc(t_mt_kept, 1)

            @block.tensor
            def _(pe):
                pe.wait_ge(t_diag, 1)
                pe.wait_ge(t_loaded, 16 * 8)
                for n in range(NB):
                    nc.tensor.matmul(banks[:, n, 0:CH], diag[:, n, :], wp[:, n % PAIRS, :],
                                     start=True, stop=True).then_inc(t_mt, 1)

            @block.vector
            def _(dve):
                count = [0]

                def then_wait(instruction):
                    count[0] += 1
                    instruction.then_inc(t_chain, 1)
                    dve.wait_ge(t_chain, count[0])

                def settle(instructions):
                    for i in instructions:
                        i.then_inc(t_chain, 1)
                        count[0] += 1
                    dve.wait_ge(t_chain, count[0])

                settle([nc.vector.memset(a[:], 0.0) for a in (wp, qn, qk, diag)])
                dve.sem_inc(t_zeroed, 1)
                then_wait(nc.vector.reduce_sum(rn[:], squares[:].rearrange("p b t c -> p (b t) c"), AX_X))
                nc.vector.tensor_scalar(ssq[:], rn[:], 1e-24, None, ALU.max).then_inc(t_root, 1)
                dve.wait_ge(t_root, 2)
                then_wait(nc.vector.reciprocal(nt1[:], nt0[:]))
                then_wait(nc.vector.tensor_tensor(nt0[:], nt1[:], nt1[:], ALU.mult))
                then_wait(nc.vector.tensor_tensor(rn[:], nt0[:], ssq[:], ALU.mult))
                then_wait(nc.vector.tensor_scalar(nt0[:], rn[:], -0.5, 1.5, ALU.mult, ALU.add))
                nc.vector.tensor_tensor(rn[:], nt0[:], nt1[:], ALU.mult).then_inc(t_norm, 1)
                dve.wait_ge(t_loaded, 16 * 8)
                dve.wait_ge(t_back, 16 * 5 * B)
                knv = kn[:].rearrange("p b r d -> p (b r) d")
                dve.wait_ge(t_moved, 16 * (B + 2 * NB))
                then_wait(nc.vector.tensor_tensor(scaled[:], qk[:], knv, ALU.mult))
                settle([nc.vector.tensor_scalar(logits[:, n, :], scaled[:, n, :], qn[:, n // PAIRS, n % PAIRS:n % PAIRS + 1],
                                                temp[:, n % PAIRS:n % PAIRS + 1], ALU.mult, ALU.mult) for n in range(NB)])
                for e in range(5):
                    now = logits if e == 0 else left
                    settle([nc.vector.max(tops[:, n, 8 * e:8 * e + 8], now[:, n, :]) for n in range(NB)])
                    if e < 4:
                        settle([nc.vector.match_replace(left[:, n, :], tops[:, n, 8 * e:8 * e + 8], now[:, n, :], LOWEST)
                                for n in range(NB)])
                nc.vector.tensor_scalar(lowered[:], tops[:, :, 0], -1.0, None, ALU.mult).then_inc(t_exp, 1)
                dve.wait_ge(t_exp, 2)
                settle([nc.vector.scalar_tensor_tensor(masked[:, i, n, :], logits[:, n, :], tops[:, n, k - 1:k],
                                                       expd[:, n, :], ALU.is_ge, ALU.mult)
                        for i, k in enumerate(TOPK) for n in range(NB)])
                then_wait(nc.vector.reduce_sum(sums[:].rearrange("p a n -> p (a n)"),
                                               masked[:].rearrange("p a n d -> p (a n) d"), AX_X))
                then_wait(nc.vector.reciprocal(shares[:], sums[:]))
                settle([nc.vector.tensor_scalar(sums[:, i, :], shares[:, i, :], gains[:, i:i + 1], None, ALU.mult)
                        for i in range(K4)])
                settle([nc.vector.tensor_scalar(mixed[:, n, :], masked[:, 0, n, :], sums[:, 0, n:n + 1], None, ALU.mult)
                        for n in range(NB)])
                for i in range(1, K4):
                    settle([nc.vector.scalar_tensor_tensor(mixed[:, n, :], masked[:, i, n, :], sums[:, i, n:n + 1],
                                                           mixed[:, n, :], ALU.mult, ALU.add) for n in range(NB)])
                settle([nc.vector.tensor_copy(diag[s * SLOT:s * SLOT + HC, :, s * SLOT:s * SLOT + HC],
                                              mixed[s * SLOT:s * SLOT + HC]) for s in range(2)])
                dve.sem_inc(t_diag, 1)

        with ExitStack() as ctx:
            def sb(name, shape, dtype=F32):
                return ctx.enter_context(nc.sbuf_tensor(name, shape, dtype))

            def sem(name):
                return ctx.enter_context(nc.semaphore(name))

            mix = sb("mix", [P, B, T, CH])
            vs = sb("vs", [P, 2, T, CW])
            mix_high, mix_low = sb("mix_high", [P, B, T, CH], F32R), sb("mix_low", [P, B, T, CH], F32R)
            v_high, v_low = sb("v_high", [P, 2, T, CW], F32R), sb("v_low", [P, 2, T, CW], F32R)
            xs = sb("p_x", [P, 2, T, CW])
            partials = sb("p_partials", [P, B, C * T * 12])
            up = [banks[:, 2 * i:2 * i + 2, :].rearrange("p a n -> p (a n)") for i in range(2)]
            mix_loaded, passed = sem("p_mix"), sem("p_passed")
            v_loaded, x_loaded, x1_stored = ([sem(f"p_{n}{i}") for i in range(2)] for n in ("v", "x", "x1"))
            mix_split = sem("p_mix_split")
            high_ready = sem("p_high")
            v_split = sem("p_split")
            mixed_ready = sem("p_mixed")
            x1_ready = sem("p_x1_ready")
            counted = sem("p_counted")
            block = ctx.enter_context(nc.Block())
            vector, tensor, scalar = norm_coefficients(nc, ctx, "gn1", partials, group_avg,
                                                       banks[:, 7, :], gn1)

            @block.sync
            def _(sp):
                for b in range(B):
                    sp.dma_start(mix[:, b], mix_d[b].rearrange("(k p) o -> p k o", p=P)).then_inc(mix_loaded, 16)

                def load_v(b, c, s):
                    after(sp, v_split, (b * C + c - 1) * T)
                    end_waits(sp, passed)
                    sp.dma_start(vs[:, s], v_d[b].rearrange("t p n -> p t n")[:, :, bass.ds(c * CW + W, CW)]
                                 ).then_inc(v_loaded[s], 16)

                load_v(0, 0, 0)
                for b in range(B):
                    def load(c, s):
                        i = b * C + c
                        if not (isinstance(c, int) and c == C - 1):
                            load_v(b, c + 1, 1 - s)
                        elif b + 1 < B:
                            load_v(b + 1, 0, 0)
                        after(sp, counted, (i - 1) * T)
                        end_waits(sp, passed)
                        after(sp, x1_stored[s], (b * C + c - s) * 8)
                        end_waits(sp, passed)
                        sp.dma_start(xs[:, s], xv[b][:, :, bass.ds(c * CW, CW)]).then_inc(x_loaded[s], 16)
                    over_chunks(sp, C, load)

            @block.tensor
            def _(pe):
                pe.wait_ge(mix_split, 2)
                for b in range(B):
                    def chunk(c, s):
                        pe.wait_ge(v_split, (b * C + c + 1) * T)
                        for m in range(T):
                            i = (b * C + c) * T + m
                            after(pe, x1_ready, i - 1)
                            for h in range(2):
                                for k in range(T):
                                    for j, (w, v) in enumerate(((mix_high, v_high), (mix_low, v_high), (mix_high, v_low))):
                                        last = nc.tensor.matmul(
                                            up[(s * T + m) % 2][:, h * HALF:(h + 1) * HALF],
                                            w[:, b, k, m * P:(m + 1) * P], v[:, s, k, h * HALF:(h + 1) * HALF],
                                            start=(k == 0 and j == 0), stop=(k == T - 1 and j == 2))
                            last.then_inc(mixed_ready, 1)
                    over_chunks(pe, C, chunk)
                tensor(pe)

            @block.scalar
            def _(act):
                for b in range(B):
                    def store(c, s):
                        act.wait_ge(x1_ready, (b * C + c + 1) * T)
                        end_waits(act, passed)
                        act.dma_start(x1_d[b][:, :, bass.ds(c * CW, CW)], xs[:, s]).then_inc(x1_stored[s], 16)
                    over_chunks(act, C, store)
                for s in range(2):
                    act.wait_ge(x1_stored[s], B * C * 8)
                scalar(act)

            @block.gpsimd
            def _(pool):
                for b in range(B):
                    def split_low(c, s):
                        i = b * C + c
                        pool.wait_ge(high_ready, i + 1)
                        after(pool, mixed_ready, (i - 1) * T)
                        for k in range(T):
                            nc.gpsimd.tensor_tensor(v_low[:, s, k], vs[:, s, k], v_high[:, s, k].bitcast(F32),
                                                    ALU.subtract).then_inc(v_split, 1)
                    over_chunks(pool, C, split_low)

            @block.vector
            def _(dve):
                dve.wait_ge(mix_loaded, 16 * B)
                nc.vector.tensor_copy(mix_high[:], mix[:]).then_inc(mix_split, 1)
                dve.wait_ge(mix_split, 1)
                nc.vector.tensor_tensor(mix_low[:], mix[:], mix_high[:].bitcast(F32), ALU.subtract).then_inc(mix_split, 1)

                def split_high(b, c, s):
                    i = b * C + c
                    dve.wait_ge(v_loaded[s], (i - s) * 8 + 16)
                    after(dve, mixed_ready, (i - 1) * T)
                    nc.vector.tensor_copy(v_high[:, s], vs[:, s]).then_inc(high_ready, 1)

                split_high(0, 0, 0)
                for b in range(B):
                    def chunk(c, s):
                        if not (isinstance(c, int) and c == C - 1):
                            split_high(b, c + 1, 1 - s)
                        elif b + 1 < B:
                            split_high(b + 1, 0, 0)
                        dve.wait_ge(x_loaded[s], (b * C + c - s) * 8 + 16)
                        for m in range(T):
                            i = (b * C + c) * T + m
                            dve.wait_ge(mixed_ready, i + 1)
                            nc.vector.tensor_tensor(xs[:, s, m, :], up[(s * T + m) % 2], xs[:, s, m, :],
                                                    ALU.add).then_inc(x1_ready, 1)
                            dve.wait_ge(x1_ready, i + 1)
                            for h in range(2):
                                last = nc.vector.bn_stats(
                                    partials[:, b, bass.ds(c * (T * 12) + (m * 2 + h) * 6, 6)],
                                    xs[:, s, m, h * HALF:(h + 1) * HALF])
                            last.then_inc(counted, 1)
                    over_chunks(dve, C, chunk)
                dve.wait_ge(counted, B * C * T)
                vector(dve)

        with ExitStack() as ctx:
            def sb(name, shape, dtype=F32):
                return ctx.enter_context(nc.sbuf_tensor(name, shape, dtype))

            def sem(name):
                return ctx.enter_context(nc.semaphore(name))

            NC = C + 1
            H2 = CH // 2
            REST = H2 - P
            wi_high, wi_low = sb("wi_high", [P, T, CH], F32R), sb("wi_low", [P, T, CH], F32R)
            wo = sb("wo", [P, 2, CH])
            taps = sb("taps1", [P, T, 9])
            forward, inverse = sb("forward", [P, P]), sb("inverse", [P, P])
            half_filter = sb("half_filter", [R * (R // 2 + 1), CH])
            spread = sb("spread", [R * (R // 2 + 1), P])
            filt_sb = sb("filt_sb", [P, CH])
            xw = sb("f_xw", [P, T, CW])
            x_high, x_low = sb("f_high", [P, 2, T, CW], F32R), sb("f_low", [P, 2, T, CW], F32R)
            xr = sb("f_xr", [P, 2, T, CW])
            pixels = sb("pixels", [P, 2, CH])
            spectra = sb("spectra", [P, 2, CH])
            u = sb("f_u", [P, 2, T, UR, UW])
            z = sb("f_z", [P, T, 2, CW])
            y = sb("f_y", [P, 2, T, CW])
            aside = sb("aside", [REST, CW])

            f_weights, filter_ready, f_cleared = sem("f_weights"), sem("f_filter"), sem("f_cleared")
            passed = sem("f_passed")
            wi_split = sem("f_wi_split")
            x_loaded = sem("f_x")
            r_loaded = [sem("f_r0"), sem("f_r1")]
            o_stored = [sem("f_o0"), sem("f_o1")]
            normalised = sem("f_normalised")
            high_ready = sem("f_high_ready")
            xn_ready = sem("f_xn_ready")
            s1_ready = sem("f_s1")
            pixels_kept = sem("f_pixels")
            coef_ready = sem("f_coef")
            filtered = sem("f_filtered")
            inv_ready = sem("f_inv")
            u_written = sem("f_u_written")
            window_ready = sem("f_window")
            products = sem("f_products")
            added = sem("f_added")
            early_taps = sem("f_early_taps")
            late_taps = sem("f_late_taps")
            y_ready = sem("f_y_ready")
            gelu_done = sem("f_gelu")
            gated = sem("f_gated")
            out_ready = sem("f_out")
            summed = sem("f_summed")
            block = ctx.enter_context(nc.Block())
            wi_raw = z[:].rearrange("p t b n -> p (t b n)")[:, 0:T * CH].rearrange("p (t o) -> p t o", t=T)
            CHAIN = len(DVE_TAPS)
            EARLY = CHAIN // 2
            s1_ps = [banks[:, i, 0:CH] for i in (0, 1)]
            coef_ps = [banks[:, i, 0:CH] for i in (2, 3)]
            inv_ps = [banks[:, i, 0:CH] for i in (4, 5)]
            COEF_LAG, INV_LAG = 2, 4
            OUTS = 2 * T
            OUT_AT, OUT_LATE = {7: [0]}, {0: [1], 1: [2], 2: [3], 3: [4], 4: [5]}
            SUM_AT, SUM_LATE = {}, {0: [0], 1: [1], 2: [2], 3: [3], 4: [4], 5: [5]}
            PRODUCTS_AT = {4: [(0, 0), (0, 1), (0, 2)], 5: [(1, 0)], 6: [(1, 1), (1, 2)], 7: [(2, 0), (2, 1), (2, 2)]}
            TAPS_AHEAD, TAPS_BEHIND = {6: 4, 7: 3}, {0: 3, 1: 3, 2: 3, 3: 2}
            GELU_AT, ASIDE_AT, NORMALISE_AT, GATE_AT = 2, 4, 5, 5
            HIGH_AT = [1, 2, 3]

            def shifted(t, s, tap, rows):
                dy, dx = tap // 3, tap % 3
                return u[:, s, t, dy:dy + rows, dx:dx + W]

            def rows_of(ap, rows):
                return ap[:, 0:rows * W].rearrange("p (r w) -> p r w", w=W)

            def over_slots(engine, body):
                over_chunks(engine, C, body, alone=2)
                for k in range(C, C + 4):
                    body(k, k % 2)

            def alive(k, chunk, end):
                return not isinstance(k, int) or 0 <= chunk < end

            def block_of(k, j):
                return alive(k, k if j >= 0 else k - 1, C)

            def stored(b, i, c=0, s=0):
                return (b * (C // 2 + (1 - i)) * 16) + (c - s) * 8

            def blocked(ap):
                return ap.rearrange("p (r j w) -> p r j w", r=R, w=BLK)

            def in_blocks(ap):
                return ap.rearrange("p (j r w) -> p r j w", r=R, w=BLK)

            def height(k, chunk):
                return 1 if isinstance(k, int) and chunk == C else R

            @block.sync
            def _(sp):
                loads = [(wi_raw, win.rearrange("(p t) o -> p t o", t=T)), (wo[:, 0, :], wout[0:P]),
                         (wo[0:REST, 1, :], wout[P:H2]), (taps[:], wdw1.rearrange("(t p) k -> p t k", p=P)),
                         (forward[:], forward_in), (inverse[:], inverse_in),
                         (half_filter[:], filt), (spread[:], spread_in)]
                for to, source in loads:
                    sp.dma_start(to, source).then_inc(f_weights, 16)
                sp.wait_ge(f_cleared, 2)

                def load(b, c):
                    after(sp, xn_ready, (b * C + c) * T)
                    end_waits(sp, passed)
                    sp.dma_start(xw[:], x1_d[b][:, :, bass.ds(c * CW, CW)]).then_inc(x_loaded, 16)

                load(0, 0)
                load(0, 1)
                for b in range(B):
                    def slot(k, s):
                        if alive(k, k + 2, C):
                            load(b, k + 2)
                        elif k in (C, C + 2) and b + 1 < B:
                            load(b + 1, (k - C) // 2)
                        if alive(k, k - 3, NC):
                            rows = height(k, k - 3)
                            sp.wait_ge(summed, (b * NC + k - 2) * OUTS)
                            end_waits(sp, passed)
                            if isinstance(k, int) and k == 3:
                                sp.dma_start(ov[b][:, :, 0:CW - W], xr[:, 1 - s, :, W:]).then_inc(o_stored[1 - s], 16)
                            else:
                                sp.dma_start(ov[b][:, :, bass.ds((k - 3) * CW - W, rows * W)],
                                             xr[:, 1 - s, :, 0:rows * W]).then_inc(o_stored[1 - s], 16)
                        if alive(k, k - 1, NC):
                            rows = height(k, k - 1)
                            after(sp, o_stored[1 - s], stored(b, 1 - s, k - 1, 1 - s))
                            end_waits(sp, passed)
                            if isinstance(k, int) and k == 1:
                                sp.dma_start(xr[:, 1 - s, :, W:], x1_d[b][:, :, 0:CW - W]).then_inc(r_loaded[1 - s], 16)
                            else:
                                sp.dma_start(xr[:, 1 - s, :, 0:rows * W],
                                             x1_d[b][:, :, bass.ds((k - 1) * CW - W, rows * W)]).then_inc(r_loaded[1 - s], 16)
                    over_slots(sp, slot)
                for i in range(2):
                    sp.wait_ge(o_stored[i], stored(B, i))

            @block.tensor
            def _(pe):
                pe.wait_ge(f_weights, 16 * 8)
                nc.tensor.matmul(banks[:, 7, 0:CH], spread[:], half_filter[:], start=True, stop=True).then_inc(filter_ready, 1)
                pe.wait_ge(filter_ready, 2)
                pe.wait_ge(wi_split, 2)
                for b in range(B):
                    def slot(k, s):
                        if alive(k, k, C):
                            pe.wait_ge(xn_ready, (b * C + k + 1) * T)
                        for j in range(NBLK):
                            q = (b * C + k) * NBLK + j
                            if block_of(k, j):
                                after(pe, pixels_kept, q - 1)
                                for t in range(T):
                                    for i, (xp, w) in enumerate(((x_high, wi_high), (x_low, wi_high), (x_high, wi_low))):
                                        last = nc.tensor.matmul(s1_ps[j % 2], xp[:, s, t, j * P:(j + 1) * P], w[:, t, :],
                                                                start=(t == 0 and i == 0), stop=(t == T - 1 and i == 2))
                                last.then_inc(s1_ready, 1)
                            if block_of(k, j - COEF_LAG):
                                p, slot_of = q - COEF_LAG, (j - COEF_LAG) % 2
                                pe.wait_ge(pixels_kept, p + 1)
                                after(pe, filtered, p - 1)
                                nc.tensor.matmul(coef_ps[slot_of], forward[:], pixels[:, slot_of, :],
                                                 start=True, stop=True).then_inc(coef_ready, 1)
                            if block_of(k, j - INV_LAG):
                                p, slot_of = q - INV_LAG, (j - INV_LAG) % 2
                                pe.wait_ge(filtered, p + 1)
                                after(pe, u_written, p - 1)
                                for t in range(T):
                                    last = nc.tensor.matmul(
                                        inv_ps[slot_of][:, t * P:(t + 1) * P], spectra[:, slot_of, t * P:(t + 1) * P],
                                        inverse[:], start=True, stop=True)
                                last.then_inc(inv_ready, 1)
                            for chunk, at, halves in ((k - 2, s, OUT_AT.get(j, [])), (k - 3, 1 - s, OUT_LATE.get(j, []))):
                                for w in halves if alive(k, chunk, NC) else []:
                                    g = b * NC + chunk
                                    m, h = w // 2, w % 2
                                    n = HALF if height(k, chunk) == R else W
                                    from_ = 0 if n == W else h * HALF
                                    if w == 0:
                                        pe.wait_ge(gated, g + 1)
                                    after(pe, summed, g * OUTS + w - 1)
                                    to = banks[:, 6 + w % 2, 0:n]
                                    nc.tensor.matmul(to, wo[:, 0, m * P:(m + 1) * P], y[:, at, 0, from_:from_ + n],
                                                     start=True, stop=False)
                                    nc.tensor.matmul(to, wo[0:REST, 1, m * P:(m + 1) * P], y[0:REST, at, 2, from_:from_ + n],
                                                     start=False, stop=True).then_inc(out_ready, 1)
                    over_slots(pe, slot)

            @block.scalar
            def _(act):
                act.wait_ge(filter_ready, 1)
                nc.scalar.copy(filt_sb[:], banks[:, 7, 0:CH]).then_inc(filter_ready, 1)
                act.wait_ge(f_weights, 16 * 8)
                act.wait_ge(f_cleared, 2)
                act.wait_ge(wi_split, 2)

                def split_high(b, c, s, t):
                    act.wait_ge(normalised, b * C + c + 1)
                    after(act, s1_ready, (b * C + c - 1) * NBLK)
                    nc.scalar.copy(in_blocks(x_high[:, s, t, :]), blocked(xw[:, t, :])).then_inc(high_ready, 1)

                for t in range(T):
                    split_high(0, 0, 0, t)
                for b in range(B):
                    def multiply(k, s, t, i):
                        if not alive(k, k - 1, NC):
                            return
                        rows = height(k, k - 1)
                        g = b * NC + k - 1
                        n = g * T + t
                        if t == 0 and i == 0:
                            act.wait_ge(u_written, (b * C + k) * NBLK if rows == R else (b + 1) * C * NBLK)
                            act.wait_ge(window_ready, g + 1)
                            after(act, out_ready, (g - 1) * OUTS if alive(k, k - 3, NC) else b * NC * OUTS)
                        if i == 0:
                            after(act, added, 2 * (n - T + 1))
                        to, tap = y[:, 1 - s, t, :] if i == 0 else z[:, t, i - 1, :], ACT_TAPS[i]
                        nc.scalar.activation(rows_of(to, rows), shifted(t, 1 - s, tap, rows), ACT.Copy,
                                             scale=taps[:, t, tap:tap + 1]).then_inc(products, 1)

                    def slot(k, s):
                        for j in range(NBLK):
                            q = (b * C + k) * NBLK + j
                            if block_of(k, j):
                                act.wait_ge(s1_ready, q + 1)
                                after(act, coef_ready, q - 1)
                                nc.scalar.copy(pixels[:, j % 2, :], s1_ps[j % 2]).then_inc(pixels_kept, 1)
                            if block_of(k, j - INV_LAG):
                                if j == INV_LAG:
                                    past = 0 if isinstance(k, int) and k == 0 else 1
                                    after(act, y_ready, (b * NC + k - past) * T)
                                    after(act, window_ready, b * NC + k)
                                act.wait_ge(inv_ready, q - INV_LAG + 1)
                                at = 1 + (j - INV_LAG) % NBLK * BLK
                                nc.scalar.copy(u[:, s if j >= INV_LAG else 1 - s, :, 2:UR, at:at + BLK],
                                               inv_ps[(j - INV_LAG) % 2].rearrange("p (t r w) -> p t r w", t=T, r=R)
                                               ).then_inc(u_written, 1)
                            for t, i in PRODUCTS_AT.get(j, []):
                                multiply(k, s, t, i)
                            if j in HIGH_AT:
                                t = HIGH_AT.index(j)
                                if alive(k, k + 1, C):
                                    split_high(b, k + 1, 1 - s, t)
                                elif isinstance(k, int) and k == C + 1 and b + 1 < B:
                                    split_high(b + 1, 0, 0, t)
                            g = b * NC + k - 2
                            n = height(k, k - 2) * W
                            if j == GELU_AT and alive(k, k - 2, NC):
                                act.wait_ge(y_ready, g * T + 1)
                                nc.scalar.activation(y[:, s, 0, 0:n], y[:, s, 0, 0:n], ACT.Gelu)
                            if j == ASIDE_AT and alive(k, k - 2, NC):
                                act.wait_ge(y_ready, (g + 1) * T)
                                nc.scalar.activation(y[0:REST, s, 2, 0:n], y[0:REST, s, 2, 0:n], ACT.Gelu)
                                after(act, gated, g)
                                nc.scalar.copy(aside[:, 0:n], y[REST:2 * REST, s, 2, 0:n]).then_inc(gelu_done, 1)
                    over_slots(act, slot)

            @block.gpsimd
            def _(pool):
                nc.gpsimd.memset(u[:], 0.0).then_inc(f_cleared, 1)
                nc.gpsimd.memset(xr[:], 0.0).then_inc(f_cleared, 1)
                pool.wait_ge(f_cleared, 2)

                def split_low(b, c, s):
                    after(pool, s1_ready, (b * C + c - 1) * NBLK)
                    for t in range(T):
                        pool.wait_ge(high_ready, (b * C + c) * T + t + 1)
                        nc.gpsimd.tensor_tensor(in_blocks(x_low[:, s, t, :]), blocked(xw[:, t, :]),
                                                in_blocks(x_high[:, s, t, :]).bitcast(F32),
                                                ALU.subtract).then_inc(xn_ready, 1)

                split_low(0, 0, 0)
                for b in range(B):
                    def slot(k, s):
                        if alive(k, k + 1, C):
                            split_low(b, k + 1, 1 - s)
                        elif isinstance(k, int) and k == C + 1 and b + 1 < B:
                            split_low(b + 1, 0, 0)
                        if alive(k, k, NC):
                            g = b * NC + k
                            past = g if isinstance(k, int) and k == 0 else g - 1
                            after(pool, y_ready, past * T)
                            after(pool, products, past * T * 3)
                            if isinstance(k, int) and k == 0:
                                nc.gpsimd.memset(u[:, s, :, 0:2, :], 0.0).then_inc(window_ready, 1)
                            else:
                                pool.wait_ge(u_written, (b * C + k) * NBLK)
                                if height(k, k) == 1:
                                    nc.gpsimd.memset(u[:, s, :, 2, :], 0.0)
                                end_waits(pool, passed)
                                nc.gpsimd.tensor_copy(u[:, s, :, 0:2, :], u[:, 1 - s, :, R:UR, :]).then_inc(window_ready, 1)
                        if alive(k, k - 1, NC):
                            size = height(k, k - 1) * W
                            for t in range(T):
                                n = (b * NC + k - 1) * T + t
                                pool.wait_ge(products, 3 * n + 3)
                                for i in range(2):
                                    nc.gpsimd.tensor_tensor(y[:, 1 - s, t, 0:size], y[:, 1 - s, t, 0:size],
                                                            z[:, t, i, 0:size], ALU.add).then_inc(added, 1)
                                    pool.wait_ge(added, 2 * n + i + 1)
                    over_slots(pool, slot)

            @block.vector
            def _(dve):
                dve.wait_ge(f_weights, 16 * 8)
                dve.wait_ge(filter_ready, 2)
                LATE = CHAIN - EARLY - 1
                order = [(0, k) for k in range(EARLY)]
                for t in range(T):
                    for k in range(EARLY, CHAIN):
                        order.append((t, k))
                        if t + 1 < T and k - EARLY < EARLY:
                            order.append((t + 1, k - EARLY))
                assert sum(TAPS_AHEAD.values()) + sum(TAPS_BEHIND.values()) == len(order)

                nc.vector.tensor_copy(wi_high[:], wi_raw).then_inc(wi_split, 1)
                dve.wait_ge(wi_split, 1)
                nc.vector.tensor_tensor(wi_low[:], wi_raw, wi_high[:].bitcast(F32), ALU.subtract).then_inc(wi_split, 1)

                def normalise(b, c):
                    dve.wait_ge(x_loaded, 16 * (b * C + c + 1))
                    nc.vector.tensor_scalar(xw[:], xw[:], gn1[:, b, 0:1], gn1[:, b, 1:2],
                                            ALU.subtract, ALU.mult).then_inc(normalised, 1)

                normalise(0, 0)
                normalise(0, 1)
                for b in range(B):
                    def add_taps(k, chunk, s, some):
                        g = b * NC + chunk
                        rows = height(k, chunk)
                        for t, i in some:
                            n = g * T + t
                            if i == 0:
                                dve.wait_ge(added, 2 * n + 2)
                            elif i <= EARLY:
                                dve.wait_ge(early_taps, n * EARLY + i)
                            else:
                                dve.wait_ge(late_taps, n * LATE + i - EARLY)
                            done = early_taps if i < EARLY else late_taps if i < CHAIN - 1 else y_ready
                            tap = DVE_TAPS[i]
                            to = rows_of(y[:, s, t, :], rows)
                            nc.vector.scalar_tensor_tensor(to, shifted(t, s, tap, rows), taps[:, t, tap:tap + 1], to,
                                                           ALU.mult, ALU.add).then_inc(done, 1)

                    def add_residual(k, chunk, s, w):
                        g = b * NC + chunk
                        if w == 0:
                            dve.wait_ge(r_loaded[s], stored(b, s, chunk, s) + 16)
                        dve.wait_ge(out_ready, g * OUTS + w + 1)
                        if height(k, chunk) == 1 and w % 2:
                            dve.wait_ge(summed, g * OUTS + w)
                            dve.sem_inc(summed, 1)
                            return
                        n = HALF if height(k, chunk) == R else W
                        to = xr[:, s, w // 2, w % 2 * HALF:w % 2 * HALF + n]
                        nc.vector.tensor_tensor(to, banks[:, 6 + w % 2, 0:n], to, ALU.add).then_inc(summed, 1)

                    def slot(k, s):
                        for j in range(NBLK):
                            q = (b * C + k) * NBLK + j
                            for w in SUM_LATE.get(j, []) if alive(k, k - 3, NC) else []:
                                add_residual(k, k - 3, 1 - s, w)
                            for w in SUM_AT.get(j, []) if alive(k, k - 2, NC) else []:
                                add_residual(k, k - 2, s, w)
                            if block_of(k, j - COEF_LAG + 1):
                                p, slot_of = q - COEF_LAG + 1, (j - COEF_LAG + 1) % 2
                                dve.wait_ge(coef_ready, p + 1)
                                after(dve, inv_ready, p - 1)
                                nc.vector.tensor_tensor(spectra[:, slot_of, :], coef_ps[slot_of], filt_sb[:],
                                                        ALU.mult).then_inc(filtered, 1)
                            if j in TAPS_BEHIND and alive(k, k - 2, NC):
                                from_ = sum(TAPS_AHEAD.values()) + sum(n for i, n in TAPS_BEHIND.items() if i < j)
                                add_taps(k, k - 2, s, order[from_:from_ + TAPS_BEHIND[j]])
                            if j == NORMALISE_AT:
                                if alive(k, k + 2, C):
                                    normalise(b, k + 2)
                                elif k in (C, C + 2) and b + 1 < B:
                                    normalise(b + 1, (k - C) // 2)
                            if j == GATE_AT and alive(k, k - 2, NC):
                                g = b * NC + k - 2
                                size = height(k, k - 2) * W
                                dve.wait_ge(gelu_done, g + 1)
                                nc.vector.tensor_tensor(y[:, s, 0, 0:size], y[:, s, 0, 0:size], y[:, s, 1, 0:size], ALU.mult)
                                nc.vector.tensor_tensor(y[0:REST, s, 2, 0:size], y[0:REST, s, 2, 0:size],
                                                        aside[:, 0:size], ALU.mult).then_inc(gated, 1)
                            if j in TAPS_AHEAD and alive(k, k - 1, NC):
                                from_ = sum(n for i, n in TAPS_AHEAD.items() if i < j)
                                add_taps(k, k - 1, 1 - s, order[from_:from_ + TAPS_AHEAD[j]])
                    over_slots(dve, slot)


def kernel(x, L0_conv_w_qkv, L0_conv_w_dw, L0_conv_w_proj, L0_conv_temperature, L0_conv_a1, L0_conv_a2,
           L0_conv_a3, L0_conv_a4, L1_conv_fft_filter, L1_conv_w_in, L1_conv_w_dw, L1_conv_w_out):
    import concourse.bacc as _bacc
    from concourse.bass_utils import run_bass_kernel_spmd as _run

    half = CH // 2
    hidden = [*range(0, P), *range(half, half + P), *range(P, half), *range(half + P, CH)]
    columns = [T * m + t for t in range(T) for m in range(P)]
    forward, inverse, spread = spectrum_constants()
    group = (np.arange(P)[:, None] // (GROUP // T) == np.arange(P)[None, :] // (GROUP // T))
    arrays = {
        "x": x,
        "wqkv": L0_conv_w_qkv.T,
        "wdw0": L0_conv_w_dw.reshape(3 * CH, 9),
        "wproj": L0_conv_w_proj.T[:, columns],
        "temperature": L0_conv_temperature,
        "a1": L0_conv_a1, "a2": L0_conv_a2, "a3": L0_conv_a3, "a4": L0_conv_a4,
        "filt": L1_conv_fft_filter.reshape(CH, -1).T[:, hidden],
        "win": L1_conv_w_in.T[:, hidden],
        "wdw1": L1_conv_w_dw.reshape(CH, 9)[hidden],
        "wout": L1_conv_w_out.T[:, columns],
        "identity": np.eye(P, dtype=np.float32),
        "group": group.astype(np.float32) * np.float32(T / GROUP),
        "forward": forward, "inverse": inverse, "spread": spread,
    }
    arrays = {f"in_{name}": np.ascontiguousarray(a) for name, a in arrays.items()}
    nc = _bacc.Bacc("TRN2", target_bir_lowering=False, num_devices=1)
    args = [nc.dram_tensor(name, a.shape, mybir.dt.from_np(a.dtype), kind="ExternalInput").ap()
            for name, a in arrays.items()]
    out = nc.dram_tensor("out", x.shape, F32, kind="ExternalOutput").ap()
    two_layers(nc, *args, out)
    r = _run(nc, [arrays], core_ids=[0])
    return r.results[0]["out"]
```
